# Optimizing a Trainium2 kernel written in Bass

```python
import numpy as np
import jax
import jax.numpy as jnp

def _softmax(x, axis=-1):
    return jax.nn.softmax(x, axis=axis)

def _gelu(x):
    return jax.nn.gelu(x, approximate=True)

def _silu(x):
    return jax.nn.silu(x)

def _sigmoid(x):
    return jax.nn.sigmoid(x)

def _layernorm(x, axis=-1, eps=1e-05):
    m = jnp.mean(x, axis=axis, keepdims=True)
    v = jnp.var(x, axis=axis, keepdims=True)
    return (x - m) / jnp.sqrt(v + eps)

def _scatter_add(tgt, idx, src, axis=0):
    return tgt.at[idx].add(src)

def _segment_sum(src, seg, n):
    return jax.ops.segment_sum(src, seg, n)
kernel_name = 'mk_gnn_resnorm_d2_gnn_r8_dab6ae'

def setup_inputs(seed: int=0):
    np.random.seed(seed)
    _w = jnp.asarray

    def _rec_inputs():
        import jax
        import jax.numpy as jnp
        _gk = jax.random.key(seed)
        x = 0.5 + 0.2887 * jax.random.normal(jax.random.fold_in(_gk, 1), (6250, 48), jnp.float32)
        _s = jax.random.randint(jax.random.fold_in(_gk, 2), (100000,), 0, 6250, jnp.int32)
        _d = jax.random.randint(jax.random.fold_in(_gk, 3), (100000,), 0, 6250, jnp.int32)
        _loop = jnp.arange(6250, dtype=jnp.int32)
        src = jnp.concatenate([_s, _d, _loop])
        dst = jnp.concatenate([_d, _s, _loop])
        _o = jnp.argsort(dst, stable=True)
        src = src[_o]
        dst = dst[_o]
        edge_attr_40 = jax.random.uniform(jax.random.fold_in(_gk, 12), (206250, 40), jnp.float32, 0.0, 1)
        edge_weight = jax.random.uniform(jax.random.fold_in(_gk, 14), (206250,), jnp.float32, 0.0, 6.99999)
        node_type_119 = jax.random.randint(jax.random.fold_in(_gk, 15), (6250,), 0, 119, jnp.int32)
        node_vec = jax.random.uniform(jax.random.fold_in(_gk, 16), (6250,), jnp.float32, 0.0, 1.49999)
        return (x, src, dst, edge_attr_40, edge_weight, node_type_119, node_vec)
    x, src, dst, edge_attr_40, edge_weight, node_type_119, node_vec = _rec_inputs()

    def _L0_gnn_setup():
        import jax, jax.numpy as jnp
        import numpy as np
        key = jax.random.key(seed)
        k1, k2 = jax.random.split(key)
        N, C, E = (12500, 48, 200000)
        label_mat = jax.random.uniform(k1, (N, C), dtype=jnp.float32)
        edge_index = jax.random.randint(k2, (2, E), 0, N, dtype=jnp.int64)
        return {'label_mat': label_mat, 'edge_index': edge_index, 'num_nodes': N}
    _L0_gnn_all = _L0_gnn_setup()
    _L0_gnn_in = {k: v for k, v in _L0_gnn_all.items() if k in ()}
    del _L0_gnn_all

    def _L1_gnn_setup():
        import jax, jax.numpy as jnp
        import numpy as np
        CUTOFF = 6.0
        LN_EPS = 1e-05
        key = jax.random.key(seed)
        ks = jax.random.split(key, 16)
        N, E, H, R, NEL, G = (6250, 100000, 48, 40, 119, 32)
        inp = {'h': jax.random.normal(ks[0], (N, H), jnp.float32), 'edge_index': jax.random.randint(ks[1], (2, E), 0, N, jnp.int64), 'edge_attr': jax.random.uniform(ks[2], (E, R), jnp.float32), 'distances': jax.random.uniform(ks[3], (E,), jnp.float32) * 7.0, 'atom_z': jax.random.randint(ks[4], (N,), 0, NEL, jnp.int64), 'node_mult': jax.random.uniform(ks[5], (N,), jnp.float32) + 0.5, 'batch': jnp.zeros((N,), jnp.int64), 'W1': jax.random.normal(ks[6], (H, R), jnp.float32) / np.sqrt(R), 'b1': jax.random.normal(ks[7], (H,), jnp.float32) * 0.01, 'W2': jax.random.normal(ks[8], (H, H), jnp.float32) / np.sqrt(H), 'b2': jax.random.normal(ks[9], (H,), jnp.float32) * 0.01, 'emb': jax.random.normal(ks[10], (NEL, G), jnp.float32) * 0.01, 'adaptW': jax.random.normal(ks[11], (G, G), jnp.float32) * 0.01, 'gamma': jnp.ones((H,), jnp.float32), 'beta': jnp.zeros((H,), jnp.float32)}
        return inp
    _L1_gnn_all = _L1_gnn_setup()
    _L1_gnn_in = {k: v for k, v in _L1_gnn_all.items() if k in ('W1', 'b1', 'W2', 'b2', 'emb', 'adaptW', 'gamma', 'beta')}
    del _L1_gnn_all
    return {'x': x, 'src': src, 'dst': dst, 'edge_attr_40': edge_attr_40, 'edge_weight': edge_weight, 'node_type_119': node_type_119, 'node_vec': node_vec, 'L1_gnn_W1': _L1_gnn_in['W1'], 'L1_gnn_b1': _L1_gnn_in['b1'], 'L1_gnn_W2': _L1_gnn_in['W2'], 'L1_gnn_b2': _L1_gnn_in['b2'], 'L1_gnn_emb': _L1_gnn_in['emb'], 'L1_gnn_adaptW': _L1_gnn_in['adaptW'], 'L1_gnn_gamma': _L1_gnn_in['gamma'], 'L1_gnn_beta': _L1_gnn_in['beta']}

def reference(x, src, dst, edge_attr_40, edge_weight, node_type_119, node_vec, L1_gnn_W1, L1_gnn_b1, L1_gnn_W2, L1_gnn_b2, L1_gnn_emb, L1_gnn_adaptW, L1_gnn_gamma, L1_gnn_beta):
    import jax
    import jax.numpy as jnp

    def _L0_gnn_ref(label_mat, edge_index, num_nodes):
        import jax, jax.numpy as jnp
        import numpy as np
        row, col = (edge_index[0], edge_index[1])
        self_loop = jnp.arange(num_nodes, dtype=row.dtype)
        row = jnp.concatenate([row, self_loop])
        col = jnp.concatenate([col, self_loop])
        ones = jnp.ones_like(row, dtype=label_mat.dtype)
        deg = jax.ops.segment_sum(ones, row, num_segments=num_nodes)
        deg_inv_sqrt = jnp.where(deg > 0, jax.lax.rsqrt(deg), 0.0)
        norm = deg_inv_sqrt[row] * deg_inv_sqrt[col]
        msgs = label_mat[row] * norm[:, None]
        out = jax.ops.segment_sum(msgs, col, num_segments=num_nodes)
        return out

    def _L1_gnn_ref(h, edge_index, edge_attr, distances, atom_z, node_mult, batch, W1, b1, W2, b2, emb, adaptW, gamma, beta):
        import jax, jax.numpy as jnp
        import numpy as np
        CUTOFF = 6.0
        LN_EPS = 1e-05
        src, dst = (edge_index[0], edge_index[1])
        N = h.shape[0]
        gate = jax.nn.silu(edge_attr @ W1.T + b1) @ W2.T + b2
        ei = emb[atom_z[src]]
        ej = emb[atom_z[dst]]
        adapt_logit = jnp.sum(ei * (ej @ adaptW.T), axis=-1, keepdims=True)
        gate = gate + adapt_logit
        cw = jnp.where(distances < CUTOFF, 0.5 * (jnp.cos(jnp.pi * distances / CUTOFF) + 1.0), 0.0)
        mj = node_mult[dst]
        msg = gate * h[dst] * (cw * mj)[:, None]
        agg = jax.ops.segment_sum(msg, src, num_segments=N)
        tot = jax.ops.segment_sum(mj, src, num_segments=N)
        agg = agg / jnp.clip(tot, 1e-08, None)[:, None]
        x = h + agg
        mu = jnp.mean(x, axis=-1, keepdims=True)
        var = jnp.mean(jnp.square(x - mu), axis=-1, keepdims=True)
        return (x - mu) / jnp.sqrt(var + LN_EPS) * gamma + beta
    edge_index = jnp.stack([src, dst])
    batch0 = jnp.zeros((6250,), jnp.int32)
    x = _layernorm(x + _L0_gnn_ref(x, edge_index, 6250), axis=-1)
    x = _layernorm(x + _L1_gnn_ref(x, edge_index, edge_attr_40, edge_weight, node_type_119, node_vec, batch0, L1_gnn_W1, L1_gnn_b1, L1_gnn_W2, L1_gnn_b2, L1_gnn_emb, L1_gnn_adaptW, L1_gnn_gamma, L1_gnn_beta), axis=-1)
    return x

_drawn_inputs = setup_inputs


def setup_inputs(seed=0):
    import zlib

    import numpy as np

    out = dict(_drawn_inputs(seed))
    spreads = {'L1_gnn_gamma': (1.0, 0.2), 'L1_gnn_beta': (0.0, 0.1)}
    factors = {'edge_attr_40': 6.014,
     'edge_weight': 5.042,
     'node_vec': 6.575,
     'L1_gnn_W1': 3.533,
     'L1_gnn_b1': 64.0,
     'L1_gnn_W2': 3.329,
     'L1_gnn_b2': 200.0,
     'L1_gnn_emb': 64.0,
     'L1_gnn_adaptW': 64.0}
    for name, (base, spread) in spreads.items():
        noise = np.random.default_rng([zlib.crc32(name.encode()), seed]).standard_normal(out[name].shape)
        drawn = base * np.exp(spread * noise) if base else spread * noise
        out[name] = jnp.asarray(drawn.astype(out[name].dtype))
    for name, factor in factors.items():
        out[name] = (out[name] * factor).astype(out[name].dtype)
    return out
```

```python
from contextlib import ExitStack

import concourse.bass as bass
from concourse import mybir

F32 = mybir.dt.float32
BF16 = mybir.dt.bfloat16
I32 = mybir.dt.int32
U8 = mybir.dt.uint8
ALU = mybir.AluOpType
ACT = mybir.ActivationFunctionType
AX = mybir.AxisListType

P = 128
NODES = 6250
EDGES = 206250
C = 48
RA = 40
EM = 32
NEL = 119
CUTOFF = 6.0
EPS = 1e-5

NB = -(-NODES // P)
NN = NB * P
G = 16
SLOTS = 3
NT = -(-EDGES // (P * G * SLOTS)) * SLOTS
K = NT * G
RW = C + 2
RG = 16
RT = -(-(K + NB) // (2 * RG)) * 2
RC = RT * RG
RCP = -(-RC // P)
AW = 64
HG = G // 2


def bc_mid(ap, n):
    return ap.unsqueeze(1).broadcast_to([ap.shape[0], n, ap.shape[1]])


def bc_last(ap, n):
    return ap.unsqueeze(2).broadcast_to([ap.shape[0], ap.shape[1], n])


def wait_apart(e, sem, value, passed):
    e.wait_ge(sem, value)
    e.sem_inc(passed, 1)


def build(nc, x, src, dst, edge_attr, edge_weight, node_type, node_vec, W1T, b1, W2T, b2,
          emb, embT, adaptWT, gamma, beta, out):
    table0 = nc.dram_tensor("table0", (NN, EM + C), F32).ap()
    table1 = nc.dram_tensor("table1", (NN, EM + C + 1), F32).ap()
    type_rows = nc.dram_tensor("type_rows", (NEL, 2 * EM), F32).ap()
    src_emb = nc.dram_tensor("src_emb", (P, K * EM), F32).ap()
    perm0 = nc.dram_tensor("perm0", (RC * P, RW), F32).ap()
    perm1 = nc.dram_tensor("perm1", (RC * P, RW), F32).ap()
    bucket_of = nc.dram_tensor("bucket_of", (2, P * RCP), I32).ap()

    ctx = ExitStack()
    with ctx:
        def sb(name, shape, dt=F32, to=ctx):
            return to.enter_context(nc.sbuf_tensor(name, shape, dt))

        def ps(name, shape, dt=F32, to=ctx):
            return to.enter_context(nc.psum_tensor(name, shape, dt))

        def sem(name, to=ctx):
            return to.enter_context(nc.semaphore(name))

        passed = sem("passed")
        iota_f = sb("iota_f", [P, P])
        iota_p = sb("iota_p", [P, 1])
        ident = sb("ident", [P, P])
        below = sb("below", [P, P])
        ones = sb("ones", [P, P])
        iota_h = sb("iota_h", [P, P], BF16)
        zero16 = sb("zero16", [P, 512], BF16)
        src_i = sb("src_i", [P, K], I32)
        dst_i = sb("dst_i", [P, K], I32)
        pos_i = sb("pos_i", [P, K], I32)
        src_lo = sb("src_lo", [P, K])
        dst_lo = sb("dst_lo", [P, K])
        weight = sb("weight", [P, K])
        nv = sb("nv", [P, NB])
        dinv = sb("dinv", [P, NB])
        type_e = sb("type_e", [P, NB, 2 * EM])
        x1 = sb("x1", [P, NB, C])
        w1 = sb("w1", [2 * RA, 2 * C])
        w2 = sb("w2", [2 * C + 1, 2 * C])
        b1c = sb("b1c", [2 * C, 1])
        gam = sb("gam", [P, C])
        bet = sb("bet", [P, C])

        with ExitStack() as ph:
            z_i = sb("z_i", [P, NB], I32, ph)
            zeros = sb("zeros", [P, 2650], F32, ph)
            embt = sb("embt", [EM, NEL], F32, ph)
            adt = sb("adt", [EM, EM], F32, ph)
            trow = sb("trow", [NEL, 2 * EM], F32, ph)
            qps = ps("qps", [NEL, EM], F32, ph)
            loaded, types_in, consts, qready, tready, tstored = (
                sem(n, ph) for n in ("loaded", "types_in", "consts", "qready", "tready", "tstored"))
            types_got, zeroed, blank = (sem(n, ph) for n in ("types_got", "zeroed", "blank"))
            wz, wl, io = sem("wz", ph), sem("wl", ph), sem("io", ph)
            conv, sq = sem("conv", ph), sem("sq", ph)
            hi_t = sb("hi_t", [P, K], I32, ph)
            wt = sb("wt", [P, K], F32, ph)
            wi = sb("wi", [P, K], I32, ph)
            with nc.Block() as block:
                @block.sync
                def _(e):
                    e.dma_start(src_i[:, :], src).then_inc(loaded, 16)
                    e.dma_start(dst_i[:, :], dst).then_inc(loaded, 16)
                    e.dma_start(weight[:, :], edge_weight).then_inc(loaded, 16)
                    e.dma_start(x1[:, :, :], x.rearrange("(h l) c -> l h c", l=P)).then_inc(wl, 16)
                    e.dma_start(nv[:, :], node_vec).then_inc(wl, 16)
                    e.dma_start(b1c[0:C, :], b1).then_inc(wl, 16)
                    e.dma_start(b1c[C:2 * C, :], b1).then_inc(wl, 16)
                    e.dma_start(gam[:, :], gamma.broadcast_to([P, C])).then_inc(wl, 16)
                    e.dma_start(bet[:, :], beta.broadcast_to([P, C])).then_inc(wl, 16)
                    e.wait_ge(wz, 2)
                    for k in range(2):
                        e.dma_start(w1[RA * k:RA * (k + 1), C * k:C * (k + 1)], W1T).then_inc(wl, 16)
                        e.dma_start(w2[C * k:C * (k + 1), C * k:C * (k + 1)], W2T).then_inc(wl, 16)
                        e.dma_start(w2[2 * C:2 * C + 1, C * k:C * (k + 1)], b2).then_inc(wl, 16)
                    e.wait_ge(blank, 1)
                    for a in (perm0, perm1):
                        flat = a.rearrange("(p r) c -> p (r c)", p=P)
                        n = RC * RW // 2650
                        for k in range(n):
                            e.dma_start(flat[:, 2650 * k:2650 * (k + 1)], zeros[:, :]).then_inc(zeroed, 16)
                    e.wait_ge(wl, 16 * 12)
                    e.wait_ge(zeroed, 16 * 2 * (RC * RW // 2650))

                @block.scalar
                def _(e):
                    e.dma_start(z_i[:, :], node_type).then_inc(types_in, 16)
                    e.dma_start(embt[:, :], embT).then_inc(types_in, 16)
                    e.dma_start(adt[:, :], adaptWT).then_inc(types_in, 16)
                    e.dma_start(trow[:, 0:EM], emb).then_inc(types_in, 16)
                    e.wait_ge(tready, 1)
                    e.dma_start(type_rows, trow[:, :]).then_inc(tstored, 16)
                    e.wait_ge(conv, 5)
                    e.activation(wt[:, :], wt[:, :], ACT.Sin, scale=3.1415925).then_inc(sq, 1)

                @block.tensor
                def _(e):
                    e.wait_ge(types_in, 64)
                    e.matmul(qps[:, :], embt[:, :], adt[:, :], start=True, stop=True).then_inc(qready, 1)

                @block.gpsimd
                def _(e):
                    e.iota(iota_f[:, :], [[1, P]], base=0, channel_multiplier=0,
                           allow_small_or_imprecise_dtypes=True).then_inc(io, 1)
                    e.iota(iota_p[:, :], [[0, 1]], base=0, channel_multiplier=1,
                           allow_small_or_imprecise_dtypes=True).then_inc(io, 1)
                    e.memset(zeros[:, :], 0.0).then_inc(blank, 1)
                    e.wait_ge(types_in, 64)
                    e.wait_ge(tstored, 16)
                    for h in range(NB):
                        e.indirect_dma_start(out=type_e[:, h, :], out_offset=None, in_=type_rows,
                                             in_offset=bass.IndirectOffsetOnAxis(ap=z_i[:, h:h + 1], axis=0)
                                             ).then_inc(types_got, 16)
                    e.wait_ge(types_got, 16 * NB)

                @block.vector
                def _(e):
                    e.memset(w1[:, :], 0.0).then_inc(wz, 1)
                    e.memset(w2[:, :], 0.0).then_inc(wz, 1)
                    e.memset(ones[:, :], 1.0)
                    e.memset(zero16[:, :], 0.0)
                    e.wait_ge(io, 2)
                    e.tensor_scalar(ident[:, :], iota_f[:, :], iota_p[:, 0:1], None, ALU.is_equal)
                    e.tensor_scalar(below[:, :], iota_f[:, :], iota_p[:, 0:1], None, ALU.is_gt)
                    e.tensor_copy(iota_h[:, :], iota_f[:, :])
                    e.wait_ge(qready, 1)
                    e.wait_ge(types_in, 64)
                    e.tensor_copy(trow[:, EM:2 * EM], qps[:, :]).then_inc(tready, 1)
                    e.wait_ge(loaded, 48)
                    for idx, lo in ((src_i, src_lo), (dst_i, dst_lo)):
                        n = 1 if lo is src_lo else 2
                        if n == 2:
                            e.wait_ge(consts, 2)
                        e.tensor_scalar(hi_t[:, :], idx[:, :], P - 1, None, ALU.bitwise_and).then_inc(consts, 1)
                        e.wait_ge(consts, 2 * n - 1)
                        e.tensor_copy(lo[:, :], hi_t[:, :]).then_inc(consts, 1)
                    e.tensor_scalar(wt[:, :], weight[:, :], 1.0 / (2 * CUTOFF), None, ALU.mult).then_inc(conv, 1)
                    e.wait_ge(conv, 1)
                    e.tensor_copy(wi[:, :], wt[:, :]).then_inc(conv, 1)
                    e.wait_ge(conv, 2)
                    e.tensor_copy(hi_t[:, :].bitcast(F32), wi[:, :]).then_inc(conv, 1)
                    e.wait_ge(consts, 4)
                    e.wait_ge(conv, 3)
                    e.tensor_tensor(wt[:, :], wt[:, :], hi_t[:, :].bitcast(F32), ALU.subtract).then_inc(conv, 2)
                    e.wait_ge(sq, 1)
                    e.tensor_tensor(wt[:, :], wt[:, :], wt[:, :], ALU.mult).then_inc(sq, 1)
                    e.wait_ge(sq, 2)
                    e.tensor_scalar(wt[:, :], wt[:, :], -1.0, 1.0, ALU.mult, ALU.add).then_inc(sq, 1)
                    e.wait_ge(sq, 3)
                    e.scalar_tensor_tensor(weight[:, :], weight[:, :], CUTOFF, wt[:, :], ALU.is_lt, ALU.mult)

        with ExitStack() as ph:
            lo16 = sb("lo16", [P, K], BF16, ph)
            hi16 = sb("hi16", [P, K], BF16, ph)
            hi_i = sb("hi_i", [P, K], I32, ph)
            oh_lo = sb("oh_lo", [P, 2, G, P], BF16, ph)
            oh_hi = sb("oh_hi", [P, 2, G, NB], BF16, ph)
            tab = sb("tab", [P, NB, EM + C], F32, ph)
            expo = sb("expo", [P, NB], F32, ph)
            deg1 = sb("deg1", [P, NB], F32, ph)
            deg = ps("deg", [P, 512], F32, ph)
            keyed, oh_ready, oh_used, counted, degs, roots, tabbed, stored = (
                sem(n, ph) for n in ("keyed", "oh_ready", "oh_used", "counted", "degs", "roots", "tabbed",
                                     "stored"))
            with nc.Block() as block:
                @block.vector
                def _(e):
                    e.memset(expo[:, :], -0.5)
                    e.tensor_scalar(hi_i[:, :], src_i[:, :], 7, None, ALU.logical_shift_right).then_inc(keyed, 1)
                    e.tensor_copy(lo16[:, :], src_lo[:, :])
                    e.wait_ge(keyed, 1)
                    e.tensor_copy(hi16[:, :], hi_i[:, :]).then_inc(keyed, 1)
                    e.wait_ge(keyed, 2)
                    with e.Fori(0, NT // 2) as i:
                        for s in range(2):
                            t = 2 * i + s
                            e.wait_ge(oh_used, t + 1)
                            e.tensor_tensor(oh_lo[:, s], bc_mid(iota_h[:, :], G),
                                            bc_last(lo16[:, bass.ds(t * G, G)], P),
                                            ALU.is_equal).then_inc(oh_ready, 1)
                            e.tensor_tensor(oh_hi[:, s], bc_mid(iota_h[:, 0:NB], G),
                                            bc_last(hi16[:, bass.ds(t * G, G)], NB),
                                            ALU.is_equal).then_inc(oh_ready, 1)
                    e.wait_ge(counted, 1)
                    e.tensor_scalar(deg1[:, :], deg[:, 0:NB], 1.0, None, ALU.add).then_inc(degs, 1)
                    e.wait_ge(roots, 1)
                    e.tensor_copy(tab[:, :, 0:EM], type_e[:, :, 0:EM])
                    e.tensor_tensor(tab[:, :, EM:EM + C], x1[:, :, :], bc_last(dinv[:, :], C),
                                    ALU.mult).then_inc(tabbed, 1)

                @block.tensor
                def _(e):
                    e.matmul(deg[:, :], zero16[:, 0:P], zero16[:, :], start=True, stop=False,
                             skip_group_check=True).then_inc(oh_used, 2)
                    with e.Fori(0, NT // 2) as i:
                        for s in range(2):
                            e.wait_ge(oh_ready, 2 * (2 * i + s + 1))
                            for g in range(G):
                                mm = e.matmul(deg[:, 0:NB], oh_lo[:, s, g, :], oh_hi[:, s, g, :],
                                              start=False, stop=False, skip_group_check=True)
                            mm.then_inc(oh_used, 1)
                    e.matmul(deg[:, :], zero16[:, 0:P], zero16[:, :], start=False, stop=True,
                             skip_group_check=True).then_inc(counted, 1)

                @block.gpsimd
                def _(e):
                    e.wait_ge(degs, 1)
                    e.tensor_tensor(dinv[:, :], deg1[:, :], expo[:, :], ALU.pow).then_inc(roots, 1)

                @block.sync
                def _(e):
                    e.wait_ge(tabbed, 1)
                    e.dma_start(table0.rearrange("(h l) c -> l h c", l=P), tab[:, :, :]).then_inc(stored, 16)
                    e.wait_ge(stored, 16)

        def place_rows(which, node, tag):
            with ExitStack() as ph:
                key = sb("key" + tag, [P, K], BF16, ph)
                key_i = sb("key_i" + tag, [P, K], I32, ph)
                mask = sb("mask" + tag, [P, 2, K], BF16, ph)
                run = sb("run" + tag, [P, 2, K], F32, ph)
                pos = sb("pos" + tag, [P, K], F32, ph)
                cnt = sb("cnt" + tag, [P, NB], F32, ph)
                tot_i = sb("tot_i" + tag, [P, NB], I32, ph)
                chunks = sb("chunks" + tag, [P, NB], F32, ph)
                ends = sb("ends" + tag, [P, NB], F32, ph)
                start = sb("start" + tag, [P, NB], F32, ph)
                cid_i = sb("cid_i" + tag, [P, RCP], F32, ph)
                cmp = sb("cmp" + tag, [P, RCP, NB], F32, ph)
                bof = sb("bof" + tag, [P, RCP], F32, ph)
                bof_i = sb("bof_i" + tag, [P, RCP], I32, ph)
                tmp_i = sb("tmp_i" + tag, [P, K], I32, ph)
                pref = ps("pref" + tag, [P, 2, 512], F32, ph)
                v = sem("v" + tag, ph)
                cntd, summed, cid, bst = (sem(n + tag, ph) for n in ("cntd", "summed", "cid", "bst"))
                tabled = sem("tabled" + tag, ph)
                with nc.Block() as block:
                    @block.gpsimd
                    def _(e):
                        e.iota(cid_i[:, :], [[1, RCP]], base=0, channel_multiplier=RCP,
                               allow_small_or_imprecise_dtypes=True).then_inc(cid, 1)

                    @block.tensor
                    def _(e):
                        e.wait_ge(cntd, 1)
                        e.matmul(pref[:, 0, 0:NB], below[:, :], cnt[:, :], start=True, stop=True)
                        e.matmul(pref[:, 1, 0:NB], ones[:, :], cnt[:, :], start=True,
                                 stop=True).then_inc(summed, 1)

                    @block.sync
                    def _(e):
                        e.wait_ge(tabled, 1)
                        e.dma_start(bucket_of[which:which + 1, :].rearrange("o (p q) -> (o p) q", q=RCP),
                                    bof_i[:, :]).then_inc(bst, 16)
                        e.wait_ge(bst, 16)

                    @block.vector
                    def _(e):
                        steps = [0]

                        def done(ins):
                            ins.then_inc(v, 1)
                            steps[0] += 1

                        def behind(k=0):
                            e.wait_ge(v, steps[0] - k)

                        done(e.tensor_scalar(key_i[:, :], node[:, :], 7, None, ALU.logical_shift_right))
                        done(e.memset(pos[:, :], 0.0))
                        behind(1)
                        done(e.tensor_copy(key[:, :], key_i[:, :]))
                        behind()
                        for h in range(NB):
                            if h >= 2:
                                behind(1)
                            ins = e.tensor_scalar(mask[:, h % 2, :], key[:, :], float(h), 0.0, ALU.is_equal,
                                                  ALU.add, accum_out=cnt[:, h:h + 1])
                            done(ins)
                        behind()
                        e.nop().then_inc(cntd, 1)
                        e.wait_ge(summed, 1)
                        done(e.tensor_scalar(tot_i[:, :], pref[:, 1, 0:NB], float(P - 1), None, ALU.add))
                        behind()
                        done(e.tensor_scalar(tot_i[:, :], tot_i[:, :], 7, None, ALU.logical_shift_right))
                        behind()
                        done(e.tensor_copy(chunks[:, :], tot_i[:, :]))
                        behind()
                        done(e.tensor_tensor_scan(ends[:, :], chunks[:, :], chunks[:, :], 0.0, ALU.add,
                                                  ALU.bypass))
                        behind()
                        done(e.tensor_tensor(start[:, :], ends[:, :], chunks[:, :], ALU.subtract))
                        behind()
                        done(e.tensor_scalar(start[:, :], start[:, :], float(P), -1.0, ALU.mult, ALU.add))
                        behind()
                        done(e.tensor_tensor(start[:, :], start[:, :], pref[:, 0, 0:NB], ALU.add))
                        e.wait_ge(cid, 1)
                        done(e.tensor_tensor(cmp[:, :, :], bc_last(cid_i[:, :], NB), bc_mid(ends[:, :], RCP),
                                             ALU.is_ge))
                        behind()
                        done(e.tensor_reduce(bof[:, :], cmp[:, :, :], AX.X, ALU.add))
                        behind()
                        done(e.tensor_scalar(bof[:, :], bof[:, :], float(NB - 1), float(AW), ALU.min, ALU.mult))
                        behind()
                        done(e.tensor_copy(bof_i[:, :], bof[:, :]))
                        behind()
                        e.nop().then_inc(tabled, 1)
                        for h in range(NB):
                            m, r = mask[:, h % 2, :], run[:, h % 2, :]
                            done(e.tensor_scalar(mask[:, h % 2, :].bitcast(mybir.dt.uint16), key[:, :], float(h),
                                                 None, ALU.is_equal))
                            behind()
                            done(e.tensor_tensor_scan(r, m.bitcast(mybir.dt.uint16), m.bitcast(mybir.dt.uint16),
                                                      start[:, h:h + 1], ALU.add, ALU.bypass))
                            behind()
                            done(e.copy_predicated(pos[:, :], m.bitcast(mybir.dt.uint16), r))
                        behind()
                        done(e.tensor_copy(key_i[:, :], pos[:, :]))
                        behind()
                        done(e.tensor_scalar(tmp_i[:, :], key_i[:, :], P - 1, 4, ALU.bitwise_and,
                                             ALU.logical_shift_left))
                        done(e.tensor_scalar(pos_i[:, :], key_i[:, :], 7, RG - 1, ALU.logical_shift_right,
                                             ALU.bitwise_and))
                        behind()
                        done(e.tensor_tensor(pos_i[:, :], pos_i[:, :], tmp_i[:, :], ALU.bitwise_or))
                        done(e.tensor_scalar(key_i[:, :], key_i[:, :], 11, 11, ALU.logical_shift_right,
                                             ALU.logical_shift_left))
                        behind()
                        done(e.tensor_tensor(pos_i[:, :], pos_i[:, :], key_i[:, :], ALU.bitwise_or))
                        behind()

        def reduce_rows(which, perm, result, tag):
            with ExitStack() as ph:
                acc = ps("acc" + tag, [P, 7, 512], F32, ph)
                rows = sb("rows" + tag, [P, 2, RG, RW], F32, ph)
                onehot = sb("onehot" + tag, [P, 2, RG, P], F32, ph)
                btab = sb("btab" + tag, [1, P * RCP], I32, ph)
                rows_in = [sem(f"rows_in{s}" + tag, ph) for s in range(2)]
                bt_in, oh_ready, used, cleared, summed = (
                    sem(n + tag, ph) for n in ("bt_in", "oh_ready2", "used", "cleared", "summed2"))
                rows_d = perm.rearrange("(t p g) c -> t p (g c)", p=P, g=RG)
                with nc.Block() as block:
                    @block.sync
                    def _(e):
                        e.dma_start(btab[:, :], bucket_of[which:which + 1, :]).then_inc(bt_in, 16)
                        e.wait_ge(cleared, 1)
                        with e.Fori(0, RT // 2) as i:
                            for s in range(2):
                                e.wait_ge(used, 2 * i + s + 1)
                                e.dma_start(rows[:, s].rearrange("p g c -> p (g c)"),
                                            rows_d[bass.ds(2 * i + s, 1)].rearrange("o p c -> (o p) c")
                                            ).then_inc(rows_in[s], 16)
                        e.wait_ge(summed, 1)

                    @block.vector
                    def _(e):
                        with e.Fori(0, RT // 2) as i:
                            for s in range(2):
                                e.wait_ge(rows_in[s], 16 * i + 16)
                                e.wait_ge(used, 2 * i + s + 1)
                                e.tensor_tensor(onehot[:, s], bc_mid(iota_f[:, :], RG),
                                                rows[:, s, :, C:C + 1].broadcast_to([P, RG, P]),
                                                ALU.is_equal).then_inc(oh_ready, 1)
                        e.wait_ge(summed, 1)
                        e.tensor_copy(result[:, 0:48, :], acc[:, 0:6, :].rearrange(
                            "p b (k c) -> p (b k) c", c=AW)[:, :, 0:RW])
                        e.tensor_copy(result[:, 48:NB, :], acc[:, 6:7, 0:AW][:, :, 0:RW])

                    @block.tensor
                    def _(e):
                        for b in range(7):
                            e.matmul(acc[:, b, :], zero16[:, 0:P], zero16[:, :], start=True, stop=False,
                                     skip_group_check=True)
                        e.nop().then_inc(used, 2)
                        e.nop().then_inc(cleared, 1)
                        e.wait_ge(bt_in, 16)
                        flat = acc[:, :, :].rearrange("p b c -> p (b c)")
                        with e.Fori(0, RT // 2) as i:
                            for s in range(2):
                                at = [e.value_load(btab[0:1, bass.ds((2 * i + s) * RG + g, 1)], min_val=0,
                                                   max_val=(NB - 1) * AW) for g in range(RG)]
                                e.wait_ge(oh_ready, 2 * i + s + 1)
                                for g in range(RG):
                                    mm = e.matmul(flat[:, bass.ds(at[g], RW)], onehot[:, s, g, :],
                                                  rows[:, s, g, :], start=False, stop=False,
                                                  skip_group_check=True)
                                mm.then_inc(used, 1)
                        for b in range(7):
                            mm = e.matmul(acc[:, b, :], zero16[:, 0:P], zero16[:, :], start=False, stop=True,
                                          skip_group_check=True)
                        mm.then_inc(summed, 1)

        def layer_norm(e, v, steps, val, tmp, mean, var, expo, power):
            def done(ins):
                ins.then_inc(v, 1)
                steps[0] += 1
                e.wait_ge(v, steps[0])
            done(e.tensor_reduce(mean[:, :], val, AX.X, ALU.add))
            done(e.tensor_scalar(mean[:, :], mean[:, :], 1.0 / C, None, ALU.mult))
            done(e.tensor_tensor(val, val, bc_last(mean[:, :], C), ALU.subtract))
            done(e.tensor_tensor(tmp, val, val, ALU.mult))
            done(e.tensor_reduce(var[:, :], tmp, AX.X, ALU.add))
            done(e.tensor_scalar(var[:, :], var[:, :], 1.0 / C, EPS, ALU.mult, ALU.add))
            power[1] += 1
            e.nop().then_inc(power[0], 1)
            e.wait_ge(power[2], power[1])
            done(e.tensor_tensor(val, val, bc_last(mean[:, :], C), ALU.mult))

        place_rows(0, dst_i, "a")
        with ExitStack() as ph:
            slot = sb("slot0", [P, SLOTS, G, EM + RW], F32, ph)
            gidx = sb("gidx0", [P, SLOTS, G], I32, ph)
            sidx = sb("sidx0", [P, SLOTS, G], I32, ph)
            ecomp = sb("ecomp0", [P, SLOTS, G * EM], F32, ph)
            gathered = [sem(f"gathered{s}a", ph) for s in range(SLOTS)]
            scattered = [sem(f"scattered{s}a", ph) for s in range(SLOTS)]
            estored = [sem(f"estored{s}a", ph) for s in range(SLOTS)]
            idx_ready, lo_ready, compact = (sem(n + "a", ph) for n in ("idx_ready", "lo_ready", "compact"))
            with nc.Block() as block:
                @block.vector
                def _(e):
                    e.memset(slot[:, :, :, EM + C:EM + RW], 0.0).then_inc(lo_ready, 1)
                    e.wait_ge(lo_ready, 1)

                    def indices(i, s):
                        cols = bass.ds((SLOTS * i + s) * G, G)
                        if not isinstance(i, int):
                            e.wait_ge(scattered[s], 16 * G * i)
                        e.tensor_copy(gidx[:, s, :], src_i[:, cols]).then_inc(idx_ready, 1)
                        e.tensor_copy(sidx[:, s, :], pos_i[:, cols]).then_inc(idx_ready, 1)
                        e.tensor_copy(slot[:, s, :, EM + C], dst_lo[:, cols]).then_inc(idx_ready, 1)
                    for s in range(SLOTS):
                        indices(0, s)
                    with e.Fori(1, NT // SLOTS) as i:
                        for s in range(SLOTS):
                            indices(i, s)

                @block.scalar
                def _(e):
                    def compact_rows(i, s):
                        e.wait_ge(gathered[s], 16 * G * (i + 1))
                        if not isinstance(i, int):
                            e.wait_ge(estored[s], 16 * i)
                        e.activation(ecomp[:, s, :].rearrange("p (g c) -> p g c", c=EM),
                                     slot[:, s, :, 0:EM], ACT.Copy).then_inc(compact, 1)
                    for s in range(SLOTS):
                        compact_rows(0, s)
                    with e.Fori(1, NT // SLOTS) as i:
                        for s in range(SLOTS):
                            compact_rows(i, s)

                @block.sync
                def _(e):
                    with e.Fori(0, NT // SLOTS) as i:
                        for s in range(SLOTS):
                            t = SLOTS * i + s
                            e.wait_ge(compact, t + 1)
                            e.dma_start(src_emb[:, bass.ds(t * (G * EM), G * EM)], ecomp[:, s, :]
                                        ).then_inc(estored[s], 16)
                    for s in range(SLOTS):
                        e.wait_ge(estored[s], 16 * (NT // SLOTS))

                @block.gpsimd
                def _(e):
                    def gather(i, s):
                        if not isinstance(i, int) or i > 0:
                            e.wait_ge(compact, SLOTS * (i - 1) + s + 1)
                        wait_apart(e, idx_ready, 3 * (SLOTS * i + s + 1), passed)
                        for g in range(G):
                            e.indirect_dma_start(out=slot[:, s, g, 0:EM + C], out_offset=None, in_=table0,
                                                 in_offset=bass.IndirectOffsetOnAxis(ap=gidx[:, s, g:g + 1],
                                                                                     axis=0)
                                                 ).then_inc(gathered[s], 16)

                    def scatter(i, s):
                        wait_apart(e, gathered[s], 16 * G * (i + 1), passed)
                        for g in range(G):
                            e.indirect_dma_start(out=perm0,
                                                 out_offset=bass.IndirectOffsetOnAxis(ap=sidx[:, s, g:g + 1],
                                                                                      axis=0),
                                                 in_=slot[:, s, g, EM:EM + RW], in_offset=None
                                                 ).then_inc(scattered[s], 16)

                    e.wait_ge(lo_ready, 1)
                    gather(0, 0)
                    for s in range(1, SLOTS):
                        gather(0, s)
                        scatter(0, s - 1)
                    with e.Fori(1, NT // SLOTS) as i:
                        for s in range(SLOTS):
                            gather(i, s)
                            if s:
                                scatter(i, s - 1)
                            else:
                                scatter(i - 1, SLOTS - 1)
                    scatter(NT // SLOTS - 1, SLOTS - 1)
                    for s in range(SLOTS):
                        e.wait_ge(scattered[s], 16 * G * (NT // SLOTS))

        with ExitStack() as ph:
            agg = sb("agg0", [P, NB, RW], F32, ph)
            reduce_rows(0, perm0, agg, "a")
            tmp = sb("tmp0", [P, NB, C], F32, ph)
            tab = sb("tab1", [P, NB, EM + C + 1], F32, ph)
            mean, var = sb("mean0", [P, NB], F32, ph), sb("var0", [P, NB], F32, ph)
            expo = sb("expo0", [P, NB], F32, ph)
            v, ask, answer, tabbed, stored = (sem(n, ph) for n in ("v0", "ask0", "answer0", "tabbed0", "stored0"))
            with nc.Block() as block:
                @block.vector
                def _(e):
                    steps = [0]

                    def done(ins):
                        ins.then_inc(v, 1)
                        steps[0] += 1
                        e.wait_ge(v, steps[0])
                    done(e.memset(expo[:, :], -0.5))
                    done(e.tensor_tensor(tmp[:, :, :], x1[:, :, :], bc_last(dinv[:, :], C), ALU.mult))
                    done(e.tensor_tensor(tmp[:, :, :], tmp[:, :, :], agg[:, :, 0:C], ALU.add))
                    done(e.tensor_tensor(tmp[:, :, :], tmp[:, :, :], bc_last(dinv[:, :], C), ALU.mult))
                    done(e.tensor_tensor(x1[:, :, :], x1[:, :, :], tmp[:, :, :], ALU.add))
                    layer_norm(e, v, steps, x1[:, :, :], tmp[:, :, :], mean, var, expo, [ask, 0, answer])
                    done(e.tensor_copy(tab[:, :, 0:EM], type_e[:, :, EM:2 * EM]))
                    done(e.tensor_tensor(tab[:, :, EM:EM + C], x1[:, :, :], bc_last(nv[:, :], C), ALU.mult))
                    done(e.tensor_copy(tab[:, :, EM + C], nv[:, :]))
                    e.nop().then_inc(tabbed, 1)

                @block.gpsimd
                def _(e):
                    e.wait_ge(ask, 1)
                    e.tensor_tensor(mean[:, :], var[:, :], expo[:, :], ALU.pow).then_inc(answer, 1)

                @block.sync
                def _(e):
                    e.wait_ge(tabbed, 1)
                    e.dma_start(table1.rearrange("(h l) c -> l h c", l=P), tab[:, :, :]).then_inc(stored, 16)
                    e.wait_ge(stored, 16)

        place_rows(1, src_i, "b")
        with ExitStack() as ph:
            ea = sb("ea", [P, SLOTS, G * RA], F32, ph)
            es = sb("es", [P, SLOTS, G * EM], F32, ph)
            got = sb("got", [P, SLOTS, G, EM + C + 1], F32, ph)
            msg = sb("msg", [P, SLOTS, G, RW], F32, ph)
            gidx = sb("gidx1", [P, SLOTS, G], I32, ph)
            sidx = sb("sidx1", [P, SLOTS, G], I32, ph)
            ea_t = sb("ea_t", [2 * RA, 2, 512], F32, ph)
            hid = sb("hid", [2 * C + 1, 2, 512], F32, ph)
            prod = sb("prod", [P, G, EM], F32, ph)
            logit = sb("logit", [P, G], F32, ph)
            val = sb("val", [P, 2, HG, C], F32, ph)
            pt = ps("pt", [2 * RA, 2, 512], F32, ph)
            phid = ps("phid", [2 * C, 2, 512], F32, ph)
            gate = ps("gate", [P, 2, 512], F32, ph)
            gathered = [sem(f"gathered{s}b", ph) for s in range(SLOTS)]
            scattered = [sem(f"scattered{s}b", ph) for s in range(SLOTS)]
            ea_in = [sem(f"ea_in{s}", ph) for s in range(SLOTS)]
            idx_ready, ones_ready, turned, turned_sb, hidden, hidden_sb, gated, gate_used, msg_ready, own = (
                sem(n + "b", ph) for n in ("idx_ready", "ones_ready", "turned", "turned_sb", "hidden",
                                           "hidden_sb", "gated", "gate_used", "msg_ready", "own"))
            with nc.Block() as block:
                @block.sync
                def _(e):
                    def load(i, s):
                        t = SLOTS * i + s
                        if not isinstance(i, int) or i > 0:
                            e.wait_ge(msg_ready, 4 * (SLOTS * (i - 1) + s + 1))
                        e.dma_start(ea[:, s, :], edge_attr[bass.ds(t, 1)].rearrange("o p c -> (o p) c")
                                    ).then_inc(ea_in[s], 16)
                        e.dma_start(es[:, s, :], src_emb[:, bass.ds(t * (G * EM), G * EM)]).then_inc(ea_in[s], 16)
                    for s in range(SLOTS):
                        load(0, s)
                    with e.Fori(1, NT // SLOTS) as i:
                        for s in range(SLOTS):
                            load(i, s)

                @block.tensor
                def _(e):
                    e.wait_ge(ones_ready, 1)

                    def tile(i, s):
                        e.wait_ge(ea_in[s], 32 * (i + 1))
                        for hf in range(2):
                            n = 2 * (SLOTS * i + s) + hf
                            if not isinstance(i, int):
                                e.wait_ge(turned_sb, n - 1)
                            elif n >= 2:
                                e.wait_ge(turned_sb, n - 1)
                            for k in range(4):
                                g = hf * HG + 2 * k
                                mm = e.transpose(pt[:, hf, P * k:P * (k + 1)], ea[:, s, g * RA:(g + 2) * RA],
                                                 ident[:, :])
                            mm.then_inc(turned, 1)
                        for hf in range(2):
                            n = 2 * (SLOTS * i + s) + hf
                            e.wait_ge(turned_sb, n + 1)
                            if not isinstance(i, int) or n >= 2:
                                e.wait_ge(hidden_sb, n - 1)
                            e.matmul(phid[:, hf, :], w1[:, :], ea_t[:, hf, :], start=True,
                                     stop=True).then_inc(hidden, 1)
                        for hf in range(2):
                            n = 2 * (SLOTS * i + s) + hf
                            e.wait_ge(hidden_sb, n + 1)
                            if not isinstance(i, int) or n >= 2:
                                e.wait_ge(gate_used, n - 1)
                            for k in range(4):
                                mm = e.matmul(gate[:, hf, 2 * C * k:2 * C * (k + 1)],
                                              hid[:, hf, P * k:P * (k + 1)], w2[:, :], start=True, stop=True)
                            mm.then_inc(gated, 1)
                    for s in range(SLOTS):
                        tile(0, s)
                    with e.Fori(1, NT // SLOTS) as i:
                        for s in range(SLOTS):
                            tile(i, s)

                @block.scalar
                def _(e):
                    def tile(i, s):
                        for hf in range(2):
                            n = 2 * (SLOTS * i + s) + hf
                            e.wait_ge(turned, n + 1)
                            if not isinstance(i, int) or n >= 2:
                                e.wait_ge(hidden, n - 1)
                            e.activation(ea_t[:, hf, :], pt[:, hf, :], ACT.Copy).then_inc(turned_sb, 1)
                        for hf in range(2):
                            n = 2 * (SLOTS * i + s) + hf
                            e.wait_ge(hidden, n + 1)
                            if not isinstance(i, int) or n >= 2:
                                e.wait_ge(gated, n - 1)
                            e.activation(hid[0:2 * C, hf, :], phid[:, hf, :], ACT.Silu,
                                         bias=b1c[:, 0:1]).then_inc(hidden_sb, 1)
                    for s in range(SLOTS):
                        tile(0, s)
                    with e.Fori(1, NT // SLOTS) as i:
                        for s in range(SLOTS):
                            tile(i, s)

                @block.vector
                def _(e):
                    e.memset(hid[2 * C:2 * C + 1, :, :], 1.0).then_inc(ones_ready, 1)

                    def indices(i, s):
                        t = SLOTS * i + s
                        cols = bass.ds(t * G, G)
                        if not isinstance(i, int) or i > 0:
                            e.wait_ge(scattered[s], 16 * G * i)
                        e.tensor_copy(gidx[:, s, :], dst_i[:, cols]).then_inc(idx_ready, 1)
                        e.tensor_copy(sidx[:, s, :], pos_i[:, cols]).then_inc(idx_ready, 1)

                    def tile(i, s):
                        t = SLOTS * i + s
                        cols = bass.ds(t * G, G)
                        e.wait_ge(ea_in[s], 32 * (i + 1))
                        e.wait_ge(gathered[s], 16 * G * (i + 1))
                        own0 = 4 * t
                        e.tensor_tensor(prod[:, :, :], es[:, s, :].rearrange("p (g c) -> p g c", c=EM),
                                        got[:, s, :, 0:EM], ALU.mult).then_inc(own, 1)
                        e.wait_ge(own, own0 + 1)
                        e.tensor_reduce(logit[:, :], prod[:, :, :], AX.X, ALU.add).then_inc(own, 1)
                        e.wait_ge(own, own0 + 2)
                        for hf in range(2):
                            n = 2 * t + hf
                            gs = slice(hf * HG, (hf + 1) * HG)
                            e.wait_ge(gated, n + 1)
                            e.tensor_tensor(val[:, hf], gate[:, hf, 0:HG * C].rearrange("p (g c) -> p g c", c=C),
                                            bc_last(logit[:, gs], C), ALU.add).then_inc(gate_used, 1)
                        e.wait_ge(gate_used, 2 * t + 2)
                        for hf in range(2):
                            gs = slice(hf * HG, (hf + 1) * HG)
                            e.tensor_tensor(val[:, hf], val[:, hf], got[:, s, gs, EM:EM + C],
                                            ALU.mult).then_inc(own, 1)
                        e.wait_ge(own, own0 + 4)
                        for hf in range(2):
                            gs = slice(hf * HG, (hf + 1) * HG)
                            e.tensor_tensor(msg[:, s, gs, 0:C], val[:, hf],
                                            bc_last(weight[:, bass.ds(t * G + hf * HG, HG)], C),
                                            ALU.mult).then_inc(msg_ready, 1)
                        e.tensor_copy(msg[:, s, :, C], src_lo[:, cols]).then_inc(msg_ready, 1)
                        e.tensor_copy(msg[:, s, :, C + 1], got[:, s, :, EM + C]).then_inc(msg_ready, 1)
                        e.wait_ge(msg_ready, 4 * t + 2)
                    for s in range(SLOTS):
                        indices(0, s)
                    for s in range(SLOTS):
                        tile(0, s)
                    with e.Fori(1, NT // SLOTS) as i:
                        for s in range(SLOTS):
                            indices(i, s)
                        for s in range(SLOTS):
                            tile(i, s)

                @block.gpsimd
                def _(e):
                    def gather(i, s):
                        wait_apart(e, idx_ready, 2 * (SLOTS * i + s + 1), passed)
                        for g in range(G):
                            e.indirect_dma_start(out=got[:, s, g, :], out_offset=None, in_=table1,
                                                 in_offset=bass.IndirectOffsetOnAxis(ap=gidx[:, s, g:g + 1],
                                                                                     axis=0)
                                                 ).then_inc(gathered[s], 16)

                    def scatter(i, s):
                        wait_apart(e, msg_ready, 4 * (SLOTS * i + s + 1), passed)
                        for g in range(G):
                            e.indirect_dma_start(out=perm1,
                                                 out_offset=bass.IndirectOffsetOnAxis(ap=sidx[:, s, g:g + 1],
                                                                                      axis=0),
                                                 in_=msg[:, s, g, :], in_offset=None
                                                 ).then_inc(scattered[s], 16)
                    for s in range(SLOTS):
                        gather(0, s)
                    for s in range(SLOTS):
                        scatter(0, s)
                    with e.Fori(1, NT // SLOTS) as i:
                        for s in range(SLOTS):
                            gather(i, s)
                        for s in range(SLOTS):
                            scatter(i, s)
                    for s in range(SLOTS):
                        e.wait_ge(scattered[s], 16 * G * (NT // SLOTS))

        with ExitStack() as ph:
            agg = sb("agg1", [P, NB, RW], F32, ph)
            reduce_rows(1, perm1, agg, "b")
            tmp = sb("tmp1", [P, NB, C], F32, ph)
            y = sb("y1", [P, NB, C], F32, ph)
            mean, var = sb("mean1", [P, NB], F32, ph), sb("var1", [P, NB], F32, ph)
            expo = sb("expo1", [P, NB], F32, ph)
            v, ask, answer, ready, stored = (sem(n, ph) for n in ("v1", "ask1", "answer1", "ready1", "stored1"))
            with nc.Block() as block:
                @block.vector
                def _(e):
                    steps = [0]

                    def done(ins):
                        ins.then_inc(v, 1)
                        steps[0] += 1
                        e.wait_ge(v, steps[0])
                    power = [ask, 0, answer]
                    done(e.memset(expo[:, :], -0.5))
                    done(e.tensor_scalar(var[:, :], agg[:, :, C + 1], 1e-8, None, ALU.max))
                    done(e.reciprocal(mean[:, :], var[:, :]))
                    done(e.tensor_tensor(y[:, :, :], agg[:, :, 0:C], bc_last(mean[:, :], C), ALU.mult))
                    done(e.tensor_tensor(y[:, :, :], y[:, :, :], x1[:, :, :], ALU.add))
                    layer_norm(e, v, steps, y[:, :, :], tmp[:, :, :], mean, var, expo, power)
                    done(e.tensor_tensor(y[:, :, :], y[:, :, :], bc_mid(gam[:, :], NB), ALU.mult))
                    done(e.tensor_tensor(y[:, :, :], y[:, :, :], bc_mid(bet[:, :], NB), ALU.add))
                    done(e.tensor_tensor(y[:, :, :], y[:, :, :], x1[:, :, :], ALU.add))
                    layer_norm(e, v, steps, y[:, :, :], tmp[:, :, :], mean, var, expo, power)
                    e.nop().then_inc(ready, 1)

                @block.gpsimd
                def _(e):
                    for k in range(2):
                        e.wait_ge(ask, k + 1)
                        e.tensor_tensor(mean[:, :], var[:, :], expo[:, :], ALU.pow).then_inc(answer, 1)

                @block.sync
                def _(e):
                    e.wait_ge(ready, 1)
                    full = NODES // P
                    e.dma_start(out[0:full * P, :].rearrange("(h l) c -> l h c", l=P),
                                y[:, 0:full, :]).then_inc(stored, 16)
                    e.dma_start(out[full * P:NODES, :], y[0:NODES - full * P, full, :]).then_inc(stored, 16)
                    e.wait_ge(stored, 32)


def kernel(**inputs):
    import numpy as np
    import concourse.bacc as bacc
    from concourse.bass_utils import run_bass_kernel_spmd

    a = {k: np.ascontiguousarray(v) for k, v in inputs.items()}

    def padded(v, n, fill=0):
        out = np.full((n,) + v.shape[1:], fill, v.dtype)
        out[:v.shape[0]] = v
        return out

    def by_tile(v, fill=0):
        return np.ascontiguousarray(padded(v, K * P, fill).reshape(NT, P, G).transpose(1, 0, 2).reshape(P, K))

    def by_node(v):
        return np.ascontiguousarray(padded(v, NN).reshape(NB, P).T)

    f = {
        "x": padded(a["x"], NN),
        "src": by_tile(a["src"], NN - 1),
        "dst": by_tile(a["dst"], NN - 1),
        "edge_attr": padded(a["edge_attr_40"], K * P).reshape(NT, P, G * RA),
        "edge_weight": by_tile(a["edge_weight"]),
        "node_type": by_node(a["node_type_119"]),
        "node_vec": by_node(a["node_vec"]),
        "W1T": np.ascontiguousarray(a["L1_gnn_W1"].T),
        "b1": a["L1_gnn_b1"].reshape(C, 1),
        "W2T": np.ascontiguousarray(a["L1_gnn_W2"].T),
        "b2": a["L1_gnn_b2"].reshape(1, C),
        "emb": a["L1_gnn_emb"],
        "embT": np.ascontiguousarray(a["L1_gnn_emb"].T),
        "adaptWT": np.ascontiguousarray(a["L1_gnn_adaptW"].T),
        "gamma": a["L1_gnn_gamma"].reshape(1, C),
        "beta": a["L1_gnn_beta"].reshape(1, C),
    }
    nc = bacc.Bacc("TRN2", target_bir_lowering=False, num_devices=1)
    args = {k: nc.dram_tensor("in_" + k, v.shape, mybir.dt.from_np(v.dtype), kind="ExternalInput").ap()
            for k, v in f.items()}
    out = nc.dram_tensor("out_nodes", (NODES, C), F32, kind="ExternalOutput").ap()
    build(nc, out=out, **args)
    r = run_bass_kernel_spmd(nc, [{"in_" + k: v for k, v in f.items()}], core_ids=[0])
    return r.results[0]["out_nodes"]
```

```python
from contextlib import ExitStack, contextmanager

import concourse.bass as bass
from concourse import mybir

F32 = mybir.dt.float32
BF16 = mybir.dt.bfloat16
I32 = mybir.dt.int32
U16 = mybir.dt.uint16
ALU = mybir.AluOpType
ACT = mybir.ActivationFunctionType
AX = mybir.AxisListType

P = 128
NODES = 6250
EDGES = 206250
C = 48
RA = 40
EM = 32
NEL = 119
CUTOFF = 6.0
EPS = 1e-5

NB = -(-NODES // P)
NN = NB * P
G = 16
SLOTS = 3
NT = -(-EDGES // (P * G * SLOTS)) * SLOTS
K = NT * G
RW = C + 2
RG = 16
RS = 4
RT = -(-(K + NB) // (RS * RG)) * RS
RC = RT * RG
RCP = -(-RC // P)
AW = 64
HG = G // 2
TW = EM + C + 1
PB = 2
SW = PB * (NT // SLOTS)


def bc_mid(ap, n):
    return ap.unsqueeze(1).broadcast_to([ap.shape[0], n, ap.shape[1]])


def bc_last(ap, n):
    return ap.unsqueeze(2).broadcast_to([ap.shape[0], ap.shape[1], n])


def wait_apart(e, sem, value, passed):
    e.wait_ge(sem, value)
    e.sem_inc(passed, 1)


def first_turn(i):
    return isinstance(i, int) and i == 0


def build(nc, x, src, dst, edge_attr, edge_weight, node_type, node_vec, W1T, b1, W2T, b2,
          emb, embT, adaptWT, gamma, beta, out):
    table0 = nc.dram_tensor("table0", (NN, EM + C), F32).ap()
    table1 = nc.dram_tensor("table1", (NN, TW), F32).ap()
    parts1 = nc.dram_tensor("parts1", (NN + P, 3 * TW), BF16).ap()
    type_rows = nc.dram_tensor("type_rows", (NEL, 2 * EM), F32).ap()
    src_emb = nc.dram_tensor("src_emb", (P, K * EM), F32).ap()
    perm0 = nc.dram_tensor("perm0", (RC * P, RW), F32).ap()
    perm1 = nc.dram_tensor("perm1", (RC * P, RW), F32).ap()
    bucket_of = nc.dram_tensor("bucket_of", (2, P * RCP), I32).ap()

    ctx = ExitStack()
    with ctx:
        def sb(name, shape, dt=F32, to=ctx):
            return to.enter_context(nc.sbuf_tensor(name, shape, dt))

        def ps(name, shape, dt=F32, to=ctx):
            return to.enter_context(nc.psum_tensor(name, shape, dt))

        def sem(name, to=ctx):
            return to.enter_context(nc.semaphore(name))

        passed = sem("passed")
        iota_f = sb("iota_f", [P, P])
        iota_p = sb("iota_p", [P, 1])
        ident = sb("ident", [P, P])
        below = sb("below", [P, P])
        ones = sb("ones", [P, P])
        iota_h = sb("iota_h", [P, P], BF16)
        zero16 = sb("zero16", [P, 512], BF16)
        src_i = sb("src_i", [P, K], I32)
        dst_i = sb("dst_i", [P, K], I32)
        pos_i = sb("pos_i", [P, K], I32)
        start = sb("start", [P, SW])
        win_f = sb("win_f", [P, NT])
        win_i = sb("win_i", [P, NT], I32)
        near = sb("near", [P, 1], I32)
        d_off = sb("d_off", [P, K], BF16)
        src_lo = sb("src_lo", [P, K])
        dst_lo = sb("dst_lo", [P, K])
        weight = sb("weight", [P, K])
        nv = sb("nv", [P, NB])
        dinv = sb("dinv", [P, NB])
        type_e = sb("type_e", [P, NB, 2 * EM])
        x1 = sb("x1", [P, NB, C])
        src_cnt = sb("src_cnt", [P, NB])
        far_cnt = sb("far_cnt", [P, NB])
        w1 = sb("w1", [2 * RA, 2 * C])
        w2 = sb("w2", [2 * C + 1, 2 * C])
        b1c = sb("b1c", [2 * C, 1])
        gam = sb("gam", [P, C])
        bet = sb("bet", [P, C])

        zeroed = sem("zeroed")
        zeros = sb("zeros", [P, 2700])

        CLEARS = RC * RW // 2700

        def clear(e, perm, sem_):
            flat = perm.rearrange("(p r) c -> p (r c)", p=P)
            for k in range(CLEARS):
                e.dma_start(flat[:, 2700 * k:2700 * (k + 1)], zeros[:, :]).then_inc(sem_, 16)

        with ExitStack() as ph:
            z_i = sb("z_i", [P, NB], I32, ph)
            embt = sb("embt", [EM, NEL], F32, ph)
            adt = sb("adt", [EM, EM], F32, ph)
            trow = sb("trow", [NEL, 2 * EM], F32, ph)
            qps = ps("qps", [NEL, EM], F32, ph)
            loaded, types_in, consts, qready, tready, tstored = (
                sem(n, ph) for n in ("loaded", "types_in", "consts", "qready", "tready", "tstored"))
            types_got, blank = (sem(n, ph) for n in ("types_got", "blank"))
            wz, wl, io = sem("wz", ph), sem("wl", ph), sem("io", ph)
            conv, sq = sem("conv", ph), sem("sq", ph)
            hi_t = sb("hi_t", [P, K], I32, ph)
            wt = sb("wt", [P, K], F32, ph)
            wi = sb("wi", [P, K], I32, ph)
            with nc.Block() as block:
                @block.sync
                def _(e):
                    e.dma_start(src_i[:, :], src).then_inc(loaded, 16)
                    e.dma_start(dst_i[:, :], dst).then_inc(loaded, 16)
                    e.dma_start(weight[:, :], edge_weight).then_inc(loaded, 16)
                    e.dma_start(x1[:, :, :], x.rearrange("(h l) c -> l h c", l=P)).then_inc(wl, 16)
                    e.dma_start(nv[:, :], node_vec).then_inc(wl, 16)
                    e.dma_start(b1c[0:C, :], b1).then_inc(wl, 16)
                    e.dma_start(b1c[C:2 * C, :], b1).then_inc(wl, 16)
                    e.dma_start(gam[:, :], gamma.broadcast_to([P, C])).then_inc(wl, 16)
                    e.dma_start(bet[:, :], beta.broadcast_to([P, C])).then_inc(wl, 16)
                    e.wait_ge(wz, 2)
                    for k in range(2):
                        e.dma_start(w1[RA * k:RA * (k + 1), C * k:C * (k + 1)], W1T).then_inc(wl, 16)
                        e.dma_start(w2[C * k:C * (k + 1), C * k:C * (k + 1)], W2T).then_inc(wl, 16)
                        e.dma_start(w2[2 * C:2 * C + 1, C * k:C * (k + 1)], b2).then_inc(wl, 16)
                    e.wait_ge(blank, 1)
                    clear(e, perm1, zeroed)
                    e.dma_start(parts1[NN:NN + P, :], zeros[:, 0:3 * TW // 2 + 1].bitcast(BF16)[:, 0:3 * TW]
                                ).then_inc(wl, 16)
                    e.wait_ge(wl, 16 * 13)

                @block.scalar
                def _(e):
                    e.dma_start(z_i[:, :], node_type).then_inc(types_in, 16)
                    e.dma_start(embt[:, :], embT).then_inc(types_in, 16)
                    e.dma_start(adt[:, :], adaptWT).then_inc(types_in, 16)
                    e.dma_start(trow[:, 0:EM], emb).then_inc(types_in, 16)
                    e.wait_ge(tready, 1)
                    e.dma_start(type_rows, trow[:, :]).then_inc(tstored, 16)
                    e.wait_ge(conv, 5)
                    e.activation(wt[:, :], wt[:, :], ACT.Sin, scale=3.1415925).then_inc(sq, 1)

                @block.tensor
                def _(e):
                    e.wait_ge(types_in, 64)
                    e.matmul(qps[:, :], embt[:, :], adt[:, :], start=True, stop=True).then_inc(qready, 1)

                @block.gpsimd
                def _(e):
                    e.iota(iota_f[:, :], [[1, P]], base=0, channel_multiplier=0,
                           allow_small_or_imprecise_dtypes=True).then_inc(io, 1)
                    e.iota(iota_p[:, :], [[0, 1]], base=0, channel_multiplier=1,
                           allow_small_or_imprecise_dtypes=True).then_inc(io, 1)
                    e.memset(zeros[:, :], 0.0).then_inc(blank, 1)
                    e.wait_ge(types_in, 64)
                    e.wait_ge(tstored, 16)
                    for h in range(NB):
                        e.indirect_dma_start(out=type_e[:, h, :], out_offset=None, in_=type_rows,
                                             in_offset=bass.IndirectOffsetOnAxis(ap=z_i[:, h:h + 1], axis=0)
                                             ).then_inc(types_got, 16)
                    e.wait_ge(types_got, 16 * NB)

                @block.vector
                def _(e):
                    e.memset(w1[:, :], 0.0).then_inc(wz, 1)
                    e.memset(w2[:, :], 0.0).then_inc(wz, 1)
                    e.memset(ones[:, :], 1.0)
                    e.memset(zero16[:, :], 0.0)
                    e.wait_ge(io, 2)
                    e.tensor_scalar(ident[:, :], iota_f[:, :], iota_p[:, 0:1], None, ALU.is_equal)
                    e.tensor_scalar(below[:, :], iota_f[:, :], iota_p[:, 0:1], None, ALU.is_gt)
                    e.tensor_copy(iota_h[:, :], iota_f[:, :])
                    e.wait_ge(qready, 1)
                    e.wait_ge(types_in, 64)
                    e.tensor_copy(trow[:, EM:2 * EM], qps[:, :]).then_inc(tready, 1)
                    e.wait_ge(loaded, 48)
                    for idx, lo in ((src_i, src_lo), (dst_i, dst_lo)):
                        n = 1 if lo is src_lo else 2
                        if n == 2:
                            e.wait_ge(consts, 2)
                        e.tensor_scalar(hi_t[:, :], idx[:, :], P - 1, None, ALU.bitwise_and).then_inc(consts, 1)
                        e.wait_ge(consts, 2 * n - 1)
                        e.tensor_copy(lo[:, :], hi_t[:, :]).then_inc(consts, 1)
                    e.tensor_scalar(wt[:, :], weight[:, :], 1.0 / (2 * CUTOFF), None, ALU.mult).then_inc(conv, 1)
                    e.wait_ge(conv, 1)
                    e.tensor_copy(wi[:, :], wt[:, :]).then_inc(conv, 1)
                    e.wait_ge(conv, 2)
                    e.tensor_copy(hi_t[:, :].bitcast(F32), wi[:, :]).then_inc(conv, 1)
                    e.wait_ge(consts, 4)
                    e.wait_ge(conv, 3)
                    e.tensor_tensor(wt[:, :], wt[:, :], hi_t[:, :].bitcast(F32), ALU.subtract).then_inc(conv, 2)
                    e.wait_ge(sq, 1)
                    e.tensor_tensor(wt[:, :], wt[:, :], wt[:, :], ALU.mult).then_inc(sq, 1)
                    e.wait_ge(sq, 2)
                    e.tensor_scalar(wt[:, :], wt[:, :], -1.0, 1.0, ALU.mult, ALU.add).then_inc(sq, 1)
                    e.wait_ge(sq, 3)
                    e.scalar_tensor_tensor(weight[:, :], weight[:, :], CUTOFF, wt[:, :], ALU.is_lt, ALU.mult)

        with ExitStack() as ph:
            dst_f = sb("dst_f", [P, K], F32, ph)
            low, high = sb("low", [P, NT], F32, ph), sb("high", [P, NT], F32, ph)
            ends2 = sb("ends2", [P, 2], F32, ph)
            diag = sb("diag", [P, 2, NT], F32, ph)
            worst = sb("worst", [P, 1], F32, ph)
            turned = ps("turned_w", [P, 2, 512], F32, ph)
            spread_w = ps("spread_w", [P, 2, 512], F32, ph)
            v, across, spread_done = (sem(n, ph) for n in ("v_w", "across_w", "spread_done_w"))
            with nc.Block() as block:
                @block.vector
                def _(e):
                    steps = [0]

                    def done(ins):
                        ins.then_inc(v, 1)
                        steps[0] += 1
                        e.wait_ge(v, steps[0])
                    by_tile = dst_f[:, :].rearrange("p (t g) -> p t g", g=G)
                    done(e.tensor_copy(dst_f[:, :], dst_i[:, :]))
                    done(e.tensor_reduce(low[:, :], by_tile, AX.X, ALU.min))
                    done(e.tensor_reduce(high[:, :], by_tile, AX.X, ALU.max))
                    e.wait_ge(across, 2)
                    done(e.tensor_reduce(ends2[0:NT, 0:1], turned[0:NT, 0, 0:P], AX.X, ALU.min))
                    done(e.tensor_reduce(ends2[0:NT, 1:2], turned[0:NT, 1, 0:P], AX.X, ALU.max))
                    done(e.tensor_tensor(ends2[0:NT, 1:2], ends2[0:NT, 1:2], ends2[0:NT, 0:1], ALU.subtract))
                    for k in range(2):
                        done(e.tensor_scalar(diag[0:NT, k, :], ident[0:NT, 0:NT], ends2[0:NT, k:k + 1], None,
                                             ALU.mult))
                    e.wait_ge(spread_done, 2)
                    done(e.tensor_copy(win_f[:, :], spread_w[:, 0, 0:NT]))
                    done(e.tensor_copy(win_i[:, :], win_f[:, :]))
                    done(e.tensor_reduce(worst[:, :], spread_w[:, 1, 0:NT], AX.X, ALU.max))
                    done(e.tensor_scalar(near[:, :], worst[:, :], float(P), None, ALU.is_lt))
                    done(e.tensor_tensor(d_off[:, :].rearrange("p (t g) -> p t g", g=G), by_tile,
                                         bc_last(win_f[:, :], G), ALU.subtract))

                @block.tensor
                def _(e):
                    e.wait_ge(v, 3)
                    e.transpose(turned[0:NT, 0, 0:P], low[:, :], ident[:, :]).then_inc(across, 1)
                    e.transpose(turned[0:NT, 1, 0:P], high[:, :], ident[:, :]).then_inc(across, 1)
                    e.wait_ge(v, 8)
                    for k in range(2):
                        e.matmul(spread_w[:, k, 0:NT], ones[0:NT, :], diag[0:NT, k, :], start=True,
                                 stop=True).then_inc(spread_done, 1)

        with ExitStack() as ph:
            lo16 = sb("lo16", [P, K], BF16, ph)
            hi16 = sb("hi16", [P, K], BF16, ph)
            hi_i = sb("hi_i", [P, K], I32, ph)
            oh_lo = sb("oh_lo", [P, 2, G, P], BF16, ph)
            oh_hi = sb("oh_hi", [P, 2, G, NB], BF16, ph)
            tab = sb("tab", [P, NB, EM + C], F32, ph)
            expo = sb("expo", [P, NB], F32, ph)
            deg1 = sb("deg1", [P, NB], F32, ph)
            deg = ps("deg", [P, 512], F32, ph)
            cntp = ps("cntp", [P, 512], F32, ph)
            ident16 = sb("ident16", [P, P], BF16, ph)
            keyed, oh_ready, oh_used, counted, degs, roots, tabbed, stored = (
                sem(n, ph) for n in ("keyed", "oh_ready", "oh_used", "counted", "degs", "roots", "tabbed",
                                     "stored"))
            with nc.Block() as block:
                @block.vector
                def _(e):
                    e.memset(expo[:, :], -0.5)
                    e.tensor_copy(ident16[:, :], ident[:, :]).then_inc(keyed, 1)
                    e.tensor_scalar(hi_i[:, :], src_i[:, :], 7, None, ALU.logical_shift_right).then_inc(keyed, 1)
                    e.tensor_copy(lo16[:, :], src_lo[:, :])
                    e.wait_ge(keyed, 2)
                    e.tensor_copy(hi16[:, :], hi_i[:, :]).then_inc(keyed, 1)
                    e.wait_ge(keyed, 3)
                    with e.Fori(0, NT // 2) as i:
                        for s in range(2):
                            t = 2 * i + s
                            e.wait_ge(oh_used, t + 1)
                            e.tensor_tensor(oh_lo[:, s], bc_mid(iota_h[:, :], G),
                                            bc_last(lo16[:, bass.ds(t * G, G)], P),
                                            ALU.is_equal).then_inc(oh_ready, 1)
                            e.tensor_tensor(oh_hi[:, s], bc_mid(iota_h[:, 0:NB], G),
                                            bc_last(hi16[:, bass.ds(t * G, G)], NB),
                                            ALU.is_equal).then_inc(oh_ready, 1)
                    e.wait_ge(counted, 1)
                    e.tensor_scalar(deg1[:, :], deg[:, 0:NB], 1.0, None, ALU.add).then_inc(degs, 1)
                    e.tensor_copy(src_cnt[:, :], cntp[:, 0:NB])
                    e.wait_ge(roots, 1)
                    e.tensor_copy(tab[:, :, 0:EM], type_e[:, :, 0:EM])
                    e.tensor_tensor(tab[:, :, EM:EM + C], x1[:, :, :], bc_last(dinv[:, :], C),
                                    ALU.mult).then_inc(tabbed, 1)

                @block.tensor
                def _(e):
                    e.wait_ge(keyed, 1)
                    e.matmul(cntp[:, :], zero16[:, 0:P], zero16[:, :], start=True, stop=False,
                             skip_group_check=True)
                    e.matmul(deg[:, :], zero16[:, 0:P], zero16[:, :], start=True, stop=False,
                             skip_group_check=True).then_inc(oh_used, 2)
                    with e.Fori(0, NT // 2) as i:
                        for s in range(2):
                            e.wait_ge(oh_ready, 2 * (2 * i + s + 1))
                            for g in range(G):
                                e.matmul(cntp[:, 0:NB], ident16[:, :], oh_hi[:, s, g, :],
                                         start=False, stop=False, skip_group_check=True)
                                mm = e.matmul(deg[:, 0:NB], oh_lo[:, s, g, :], oh_hi[:, s, g, :],
                                              start=False, stop=False, skip_group_check=True)
                            mm.then_inc(oh_used, 1)
                    e.matmul(cntp[:, :], zero16[:, 0:P], zero16[:, :], start=False, stop=True,
                             skip_group_check=True)
                    e.matmul(deg[:, :], zero16[:, 0:P], zero16[:, :], start=False, stop=True,
                             skip_group_check=True).then_inc(counted, 1)

                @block.gpsimd
                def _(e):
                    e.wait_ge(degs, 1)
                    e.tensor_tensor(dinv[:, :], deg1[:, :], expo[:, :], ALU.pow).then_inc(roots, 1)

                @block.sync
                def _(e):
                    e.wait_ge(tabbed, 1)
                    e.dma_start(table0.rearrange("(h l) c -> l h c", l=P), tab[:, :, :]).then_inc(stored, 16)
                    e.wait_ge(stored, 16)

        @contextmanager
        def only(e, general):
            if not general:
                yield
                return
            flag = e.value_load(near[0:1, 0:1], min_val=0, max_val=1)
            with e.If(flag == 0):
                yield

        def bucket_starts(which, count, tag, general):
            with ExitStack() as ph:
                tot_i = sb("tot_i" + tag, [P, NB], I32, ph)
                chunks = sb("chunks" + tag, [P, NB], F32, ph)
                ends = sb("ends" + tag, [P, NB], F32, ph)
                cid = sb("cid" + tag, [P, RCP], F32, ph)
                cmp = sb("cmp" + tag, [P, RCP, NB], F32, ph)
                bof = sb("bof" + tag, [P, RCP], F32, ph)
                bof_i = sb("bof_i" + tag, [P, RCP], I32, ph)
                pref = ps("pref" + tag, [P, 2, 512], F32, ph)
                v = sem("vs" + tag, ph)
                summed, cid_in, bst = (sem(n + tag, ph) for n in ("summed", "cid_in", "bst"))
                with nc.Block() as block:
                    @block.gpsimd
                    def _(e):
                        e.iota(cid[:, :], [[1, RCP]], base=0, channel_multiplier=RCP,
                               allow_small_or_imprecise_dtypes=True).then_inc(cid_in, 1)

                    @block.tensor
                    def _(e):
                        with only(e, general):
                            e.matmul(pref[:, 0, 0:NB], below[:, :], count[:, :], start=True,
                                     stop=True).then_inc(summed, 1)
                            e.matmul(pref[:, 1, 0:NB], ones[:, :], count[:, :], start=True,
                                     stop=True).then_inc(summed, 1)

                    @block.sync
                    def _(e):
                        with only(e, general):
                            e.wait_ge(v, 11)
                            e.dma_start(bucket_of[which:which + 1, :].rearrange("o (p q) -> (o p) q", q=RCP),
                                        bof_i[:, :]).then_inc(bst, 16)
                            e.wait_ge(bst, 16)

                    @block.vector
                    def _(e):
                        steps = [0]

                        def done(ins):
                            ins.then_inc(v, 1)
                            steps[0] += 1
                            e.wait_ge(v, steps[0])
                        with only(e, general):
                            done(e.memset(start[:, NB:SW], 0.0))
                            e.wait_ge(summed, 2)
                            done(e.tensor_scalar(tot_i[:, :], pref[:, 1, 0:NB], float(P - 1), None, ALU.add))
                            done(e.tensor_scalar(tot_i[:, :], tot_i[:, :], 7, None, ALU.logical_shift_right))
                            done(e.tensor_copy(chunks[:, :], tot_i[:, :]))
                            done(e.tensor_tensor_scan(ends[:, :], chunks[:, :], chunks[:, :], 0.0, ALU.add,
                                                      ALU.bypass))
                            done(e.tensor_tensor(start[:, 0:NB], ends[:, :], chunks[:, :], ALU.subtract))
                            done(e.tensor_scalar(start[:, 0:NB], start[:, 0:NB], float(P), -1.0, ALU.mult,
                                                 ALU.add))
                            e.wait_ge(cid_in, 1)
                            done(e.tensor_tensor(cmp[:, :, :], bc_last(cid[:, :], NB),
                                                 bc_mid(ends[:, :], RCP), ALU.is_ge))
                            done(e.tensor_reduce(bof[:, :], cmp[:, :, :], AX.X, ALU.add))
                            done(e.tensor_scalar(bof[:, :], bof[:, :], float(NB - 1), float(AW), ALU.min,
                                                 ALU.mult))
                            done(e.tensor_copy(bof_i[:, :], bof[:, :]))
                            done(e.tensor_tensor(start[:, 0:NB], start[:, 0:NB], pref[:, 0, 0:NB], ALU.add))

        def place_bucket(e, h, tiles, done):
            key, mask, run, pos = tiles
            done(e.tensor_scalar(mask[:, :], key[:, :], iota_f[:, bass.ds(h, 1)], None, ALU.is_equal))
            done(e.tensor_tensor_scan(run[:, :], mask[:, :], mask[:, :], start[:, bass.ds(h, 1)], ALU.add,
                                      ALU.bypass))
            done(e.copy_predicated(pos[:, :], mask[:, :], run[:, :]))

        def rows_of_places(e, pos, a, b, done):
            done(e.tensor_copy(a[:, :], pos[:, :]))
            done(e.tensor_scalar(b[:, :], a[:, :], P - 1, 4, ALU.bitwise_and, ALU.logical_shift_left))
            done(e.tensor_scalar(pos_i[:, :], a[:, :], 7, RG - 1, ALU.logical_shift_right, ALU.bitwise_and))
            done(e.tensor_tensor(pos_i[:, :], pos_i[:, :], b[:, :], ALU.bitwise_or))
            done(e.tensor_scalar(a[:, :], a[:, :], 11, 11, ALU.logical_shift_right, ALU.logical_shift_left))
            done(e.tensor_tensor(pos_i[:, :], pos_i[:, :], a[:, :], ALU.bitwise_or))

        def far_places(which, node, tag):
            cnt = far_cnt
            with ExitStack() as ph:
                key = sb("keyc" + tag, [P, K], F32, ph)
                key_i = sb("keyc_i" + tag, [P, K], I32, ph)
                mask = sb("maskc" + tag, [P, K], F32, ph)
                v = sem("vc" + tag, ph)
                with nc.Block() as block:
                    @block.vector
                    def _(e):
                        def done(ins):
                            ins.then_inc(v, 1)
                            steps[0] += 1
                            e.wait_ge(v, steps[0])
                        steps = [0]
                        with only(e, True):
                            done(e.tensor_scalar(key_i[:, :], node[:, :], 7, None, ALU.logical_shift_right))
                            done(e.tensor_copy(key[:, :], key_i[:, :]))
                            for h in range(NB):
                                done(e.tensor_scalar(mask[:, :], key[:, :], float(h), 0.0, ALU.is_equal,
                                                     ALU.add, accum_out=cnt[:, h:h + 1]))
            bucket_starts(which, cnt, tag, True)
            with ExitStack() as ph:
                key = sb("key" + tag, [P, K], F32, ph)
                key_i = sb("key_i" + tag, [P, K], I32, ph)
                mask = sb("mask" + tag, [P, K], U16, ph)
                run = sb("run" + tag, [P, K], F32, ph)
                pos = sb("pos" + tag, [P, K], F32, ph)
                v = sem("v" + tag, ph)
                turn = sem("turn" + tag, ph)
                with nc.Block() as block:
                    @block.vector
                    def _(e):
                        steps = [0]

                        def done(ins):
                            ins.then_inc(v, 1)
                            steps[0] += 1
                            e.wait_ge(v, steps[0])
                        with only(e, True):
                            done(e.tensor_scalar(key_i[:, :], node[:, :], 7, None, ALU.logical_shift_right))
                            done(e.tensor_copy(key[:, :], key_i[:, :]))
                            done(e.memset(pos[:, :], 0.0))
                            with e.Fori(0, NB) as h:
                                own = [0]

                                def in_turn(ins):
                                    ins.then_inc(turn, 1)
                                    own[0] += 1
                                    e.wait_ge(turn, 3 * h + own[0])
                                    e.sem_inc(passed, 1)
                                place_bucket(e, h, (key, mask, run, pos), in_turn)
                            rows_of_places(e, pos, key_i, run[:, :].bitcast(I32), done)

        def reduce_rows(which, perm, result, tag, general):
            with ExitStack() as ph:
                acc = ps("acc" + tag, [P, 7, 512], F32, ph)
                rows = sb("rows" + tag, [P, RS, RG, RW], F32, ph)
                rest = sb("rest" + tag, [P, RS, RG, RW], F32, ph)
                part = sb("part" + tag, [P, RS, 3, RG, RW], BF16, ph)
                onehot = sb("onehot" + tag, [P, RS, RG, P], BF16, ph)
                btab = sb("btab" + tag, [1, P * RCP], I32, ph)
                rows_in = [sem(f"rows_in{s}" + tag, ph) for s in range(RS)]
                bt_in, oh_ready, used, high, rested, mid, lowp, summed = (
                    sem(n + tag, ph) for n in ("bt_in", "oh_ready2", "used", "high", "rested", "mid", "lowp",
                                               "summed2"))
                rows_d = perm.rearrange("(t p g) c -> t p (g c)", p=P, g=RG)

                def turns(e, tile):
                    for s in range(RS):
                        tile(0, s)
                    with e.Fori(1, RT // RS) as i:
                        for s in range(RS):
                            tile(i, s)

                def freed(e, i, s):
                    if not first_turn(i):
                        e.wait_ge(used, RS * (i - 1) + s + 1)

                with nc.Block() as block:
                    @block.sync
                    def _(e):
                        def load(i, s):
                            freed(e, i, s)
                            e.dma_start(rows[:, s].rearrange("p g c -> p (g c)"),
                                        rows_d[bass.ds(RS * i + s, 1)].rearrange("o p c -> (o p) c")
                                        ).then_inc(rows_in[s], 16)
                        with only(e, general):
                            e.dma_start(btab[:, :], bucket_of[which:which + 1, :]).then_inc(bt_in, 16)
                            turns(e, load)
                            e.wait_ge(summed, 1)

                    @block.scalar
                    def _(e):
                        def split(i, s):
                            e.wait_ge(rows_in[s], 16 * (i + 1))
                            freed(e, i, s)
                            e.activation(part[:, s, 0], rows[:, s], ACT.Copy).then_inc(high, 1)
                            e.wait_ge(rested, RS * i + s + 1)
                            e.activation(part[:, s, 1], rest[:, s], ACT.Copy).then_inc(mid, 1)
                        with only(e, general):
                            turns(e, split)

                    @block.gpsimd
                    def _(e):
                        def take(i, s):
                            e.wait_ge(high, RS * i + s + 1)
                            e.tensor_tensor(rest[:, s], rows[:, s], part[:, s, 0],
                                            ALU.subtract).then_inc(rested, 1)
                        with only(e, general):
                            turns(e, take)

                    @block.vector
                    def _(e):
                        def split(i, s):
                            e.wait_ge(rows_in[s], 16 * (i + 1))
                            freed(e, i, s)
                            e.tensor_tensor(onehot[:, s], bc_mid(iota_h[:, :], RG),
                                            rows[:, s, :, C:C + 1].broadcast_to([P, RG, P]),
                                            ALU.is_equal).then_inc(oh_ready, 1)

                        def low_part(i, s):
                            e.wait_ge(mid, RS * i + s + 1)
                            e.tensor_tensor(part[:, s, 2], rest[:, s], part[:, s, 1],
                                            ALU.subtract).then_inc(lowp, 1)
                        with only(e, general):
                            split(0, 0)
                            for s in range(1, RS):
                                split(0, s)
                                low_part(0, s - 1)
                            with e.Fori(1, RT // RS) as i:
                                for s in range(RS):
                                    split(i, s)
                                    if s:
                                        low_part(i, s - 1)
                                    else:
                                        low_part(i - 1, RS - 1)
                            low_part(RT // RS - 1, RS - 1)
                            e.wait_ge(summed, 1)
                            e.tensor_copy(result[:, 0:48, :], acc[:, 0:6, :].rearrange(
                                "p b (k c) -> p (b k) c", c=AW)[:, :, 0:RW])
                            e.tensor_copy(result[:, 48:NB, :], acc[:, 6:7, 0:AW][:, :, 0:RW])

                    @block.tensor
                    def _(e):
                        regs = [e.alloc_register(f"bucket{g}" + tag) for g in range(RG)]
                        flat = acc[:, :, :].rearrange("p b c -> p (b c)")

                        def tile(i, s):
                            e.load(regs, btab[0:1, bass.ds((RS * i + s) * RG, RG)])
                            at = [e.snap(r, min_val=0, max_val=(NB - 1) * AW) for r in regs]
                            e.wait_ge(oh_ready, RS * i + s + 1)
                            e.wait_ge(lowp, RS * i + s + 1)
                            for g in range(RG):
                                for k in range(3):
                                    mm = e.matmul(flat[:, bass.ds(at[g], RW)], onehot[:, s, g, :],
                                                  part[:, s, k, g, :], start=False, stop=False,
                                                  skip_group_check=True)
                            mm.then_inc(used, 1)
                        with only(e, general):
                            for b in range(7):
                                e.matmul(acc[:, b, :], zero16[:, 0:P], zero16[:, :], start=True, stop=False,
                                         skip_group_check=True)
                            e.wait_ge(bt_in, 16)
                            turns(e, tile)
                            for b in range(7):
                                mm = e.matmul(acc[:, b, :], zero16[:, 0:P], zero16[:, :], start=False,
                                              stop=True, skip_group_check=True)
                            mm.then_inc(summed, 1)

        bucket_starts(1, src_cnt, "s", False)

        def layer_norm(e, v, steps, val, tmp, mean, var, expo, power):
            def done(ins):
                ins.then_inc(v, 1)
                steps[0] += 1
                e.wait_ge(v, steps[0])
            done(e.tensor_reduce(mean[:, :], val, AX.X, ALU.add))
            done(e.tensor_scalar(mean[:, :], mean[:, :], 1.0 / C, None, ALU.mult))
            done(e.tensor_tensor(val, val, bc_last(mean[:, :], C), ALU.subtract))
            done(e.tensor_tensor(tmp, val, val, ALU.mult))
            done(e.tensor_reduce(var[:, :], tmp, AX.X, ALU.add))
            done(e.tensor_scalar(var[:, :], var[:, :], 1.0 / C, EPS, ALU.mult, ALU.add))
            power[1] += 1
            e.nop().then_inc(power[0], 1)
            e.wait_ge(power[2], power[1])
            done(e.tensor_tensor(val, val, bc_last(mean[:, :], C), ALU.mult))

        agg_ctx = ExitStack()
        accT = sb("accT", [C, NN + P], F32, agg_ctx)
        far_places(0, dst_i, "a")
        with ExitStack() as ph:
            slot = sb("slot0", [P, SLOTS, G, EM + RW], F32, ph)
            gidx = sb("gidx0", [P, SLOTS, G], I32, ph)
            sidx = sb("sidx0", [P, SLOTS, G], I32, ph)
            ecomp = sb("ecomp0", [P, SLOTS, G * EM], F32, ph)
            onehot = sb("onehot0", [P, SLOTS, G, P], F32, ph)
            key = sb("key_s", [P, K], F32, ph)
            key_i = sb("key_is", [P, K], I32, ph)
            mask = sb("mask_s", [P, K], U16, ph)
            run = sb("run_s", [P, K], F32, ph)
            pos = sb("pos_s", [P, K], F32, ph)
            sums = ps("sums0", [P, SLOTS, 512], F32, ph)
            gathered = [sem(f"gathered{s}a", ph) for s in range(SLOTS)]
            scattered = [sem(f"scattered{s}a", ph) for s in range(SLOTS)]
            estored = [sem(f"estored{s}a", ph) for s in range(SLOTS)]
            idx_ready, lo_ready, compact, oh_ready, summed, added, v, turn, cleared0 = (
                sem(n + "a", ph) for n in ("idx_ready", "lo_ready", "compact", "oh_ready_n", "summed_n",
                                           "added", "vp", "turn_p", "cleared0"))
            turns_n = NT // SLOTS
            with nc.Block() as block:
                @block.vector
                def _(e):
                    steps = [0]

                    def done(ins):
                        ins.then_inc(v, 1)
                        steps[0] += 1
                        e.wait_ge(v, steps[0])

                    def indices(i, s, far):
                        cols = bass.ds((SLOTS * i + s) * G, G)
                        if not first_turn(i):
                            e.wait_ge((scattered if far else gathered)[s], 16 * G * i)
                        e.tensor_copy(gidx[:, s, :], src_i[:, cols]).then_inc(idx_ready, 1)
                        if far:
                            e.tensor_copy(sidx[:, s, :], pos_i[:, cols]).then_inc(idx_ready, 1)
                            e.tensor_copy(slot[:, s, :, EM + C], dst_lo[:, cols]).then_inc(idx_ready, 1)

                    def near_onehot(i, s):
                        if not first_turn(i):
                            e.wait_ge(summed, SLOTS * (i - 1) + s + 1)
                        e.tensor_tensor(onehot[:, s], bc_mid(iota_f[:, :], G),
                                        bc_last(d_off[:, bass.ds((SLOTS * i + s) * G, G)], P),
                                        ALU.is_equal).then_inc(oh_ready, 1)

                    def add_window(i, s):
                        t = SLOTS * i + s
                        first = e.value_load(win_i[0:1, bass.ds(t, 1)], min_val=0, max_val=NN - 1)
                        e.wait_ge(summed, t + 1)
                        if not first_turn(i) or t > 0:
                            e.wait_ge(added, t)
                        at = accT[:, bass.ds(first, P)]
                        e.tensor_tensor(at, at, sums[0:C, s, 0:P], ALU.add).then_inc(added, 1)

                    e.memset(slot[:, :, :, EM + C:EM + RW], 0.0).then_inc(lo_ready, 1)
                    e.wait_ge(lo_ready, 1)
                    far = e.value_load(near[0:1, 0:1], min_val=0, max_val=1)
                    with e.If(far == 0):
                        for s in range(SLOTS):
                            indices(0, s, True)
                        with e.Fori(1, turns_n) as i:
                            for s in range(SLOTS):
                                indices(i, s, True)
                    with e.If(far == 1):
                        done(e.memset(accT[:, :], 0.0))
                        for s in range(SLOTS):
                            indices(0, s, False)
                        done(e.tensor_scalar(key_i[:, :], src_i[:, :], 7, None, ALU.logical_shift_right))
                        done(e.tensor_copy(key[:, :], key_i[:, :]))
                        done(e.memset(pos[:, :], 0.0))
                        for s in range(SLOTS):
                            near_onehot(0, s)
                        add_window(0, 0)
                        with e.Fori(1, turns_n) as i:
                            for s in range(SLOTS):
                                indices(i, s, False)
                                near_onehot(i, s)
                                if s < SLOTS - 1:
                                    add_window(i - 1, s + 1)
                                else:
                                    add_window(i, 0)
                            own = [0]

                            def in_turn(ins):
                                ins.then_inc(turn, 1)
                                own[0] += 1
                                e.wait_ge(turn, 3 * PB * (i - 1) + own[0])
                                e.sem_inc(passed, 1)
                            for b in range(PB):
                                place_bucket(e, PB * (i - 1) + b, (key, mask, run, pos), in_turn)
                        for s in range(1, SLOTS):
                            add_window(turns_n - 1, s)
                        rows_of_places(e, pos, key_i, run[:, :].bitcast(I32), done)

                @block.tensor
                def _(e):
                    def tile(i, s):
                        t = SLOTS * i + s
                        e.wait_ge(gathered[s], 16 * G * (i + 1))
                        e.wait_ge(oh_ready, t + 1)
                        if not first_turn(i):
                            e.wait_ge(added, SLOTS * (i - 1) + s + 1)
                        for g in range(G):
                            mm = e.matmul(sums[0:C, s, 0:P], slot[:, s, g, EM:EM + C], onehot[:, s, g, :],
                                          start=(g == 0), stop=(g == G - 1))
                        mm.then_inc(summed, 1)
                    far = e.value_load(near[0:1, 0:1], min_val=0, max_val=1)
                    with e.If(far == 1):
                        for s in range(SLOTS):
                            tile(0, s)
                        with e.Fori(1, turns_n) as i:
                            for s in range(SLOTS):
                                tile(i, s)

                @block.scalar
                def _(e):
                    def compact_rows(i, s):
                        e.wait_ge(gathered[s], 16 * G * (i + 1))
                        if not first_turn(i):
                            e.wait_ge(estored[s], 16 * i)
                        e.activation(ecomp[:, s, :].rearrange("p (g c) -> p g c", c=EM),
                                     slot[:, s, :, 0:EM], ACT.Copy).then_inc(compact, 1)
                    for s in range(SLOTS):
                        compact_rows(0, s)
                    with e.Fori(1, turns_n) as i:
                        for s in range(SLOTS):
                            compact_rows(i, s)

                @block.sync
                def _(e):
                    with only(e, True):
                        clear(e, perm0, cleared0)
                        e.wait_ge(cleared0, 16 * CLEARS)
                        e.sem_inc(lo_ready, 1)
                    with e.Fori(0, turns_n) as i:
                        for s in range(SLOTS):
                            t = SLOTS * i + s
                            e.wait_ge(compact, t + 1)
                            e.dma_start(src_emb[:, bass.ds(t * (G * EM), G * EM)], ecomp[:, s, :]
                                        ).then_inc(estored[s], 16)
                    for s in range(SLOTS):
                        e.wait_ge(estored[s], 16 * turns_n)

                @block.gpsimd
                def _(e):
                    def gather(i, s, far):
                        t = SLOTS * i + s
                        if not first_turn(i):
                            e.wait_ge(compact, t - SLOTS + 1)
                            if not far:
                                e.wait_ge(summed, t - SLOTS + 1)
                        wait_apart(e, idx_ready, (3 if far else 1) * (t + 1), passed)
                        for g in range(G):
                            e.indirect_dma_start(out=slot[:, s, g, 0:EM + C], out_offset=None, in_=table0,
                                                 in_offset=bass.IndirectOffsetOnAxis(ap=gidx[:, s, g:g + 1],
                                                                                     axis=0)
                                                 ).then_inc(gathered[s], 16)

                    def scatter(i, s):
                        wait_apart(e, gathered[s], 16 * G * (i + 1), passed)
                        for g in range(G):
                            e.indirect_dma_start(out=perm0,
                                                 out_offset=bass.IndirectOffsetOnAxis(ap=sidx[:, s, g:g + 1],
                                                                                      axis=0),
                                                 in_=slot[:, s, g, EM:EM + RW], in_offset=None
                                                 ).then_inc(scattered[s], 16)

                    e.wait_ge(lo_ready, 1)
                    far = e.value_load(near[0:1, 0:1], min_val=0, max_val=1)
                    with e.If(far == 1):
                        for s in range(SLOTS):
                            gather(0, s, False)
                        with e.Fori(1, turns_n) as i:
                            for s in range(SLOTS):
                                gather(i, s, False)
                        for s in range(SLOTS):
                            e.wait_ge(gathered[s], 16 * G * turns_n)
                    with e.If(far == 0):
                        e.wait_ge(lo_ready, 2)
                        gather(0, 0, True)
                        for s in range(1, SLOTS):
                            gather(0, s, True)
                            scatter(0, s - 1)
                        with e.Fori(1, turns_n) as i:
                            for s in range(SLOTS):
                                gather(i, s, True)
                                if s:
                                    scatter(i, s - 1)
                                else:
                                    scatter(i - 1, SLOTS - 1)
                        scatter(turns_n - 1, SLOTS - 1)
                        for s in range(SLOTS):
                            e.wait_ge(scattered[s], 16 * G * turns_n)

        agg = sb("agg0", [P, NB, RW], F32, agg_ctx)
        reduce_rows(0, perm0, agg, "a", True)
        with ExitStack() as ph:
            back = ps("back", [P, 2, 512], F32, ph)
            turned, taken = sem("turned_t", ph), sem("taken_t", ph)
            with nc.Block() as block:
                @block.tensor
                def _(e):
                    far = e.value_load(near[0:1, 0:1], min_val=0, max_val=1)
                    with e.If(far == 1):
                        for b in range(7):
                            if b >= 2:
                                e.wait_ge(taken, b - 1)
                            for k in range(min(8, NB - 8 * b)):
                                h = 8 * b + k
                                mm = e.transpose(back[:, b % 2, C * k:C * (k + 1)], accT[:, P * h:P * (h + 1)],
                                                 ident[0:C, 0:C])
                            mm.then_inc(turned, 1)

                @block.vector
                def _(e):
                    far = e.value_load(near[0:1, 0:1], min_val=0, max_val=1)
                    with e.If(far == 1):
                        for b in range(7):
                            n = min(8, NB - 8 * b)
                            e.wait_ge(turned, b + 1)
                            e.tensor_copy(agg[:, 8 * b:8 * b + n, 0:C], back[:, b % 2, 0:C * n].rearrange(
                                "p (k c) -> p k c", c=C)).then_inc(taken, 1)

        with ExitStack() as ph:
            tmp = sb("tmp0", [P, NB, C], F32, ph)
            tab = sb("tab1", [P, NB, TW], F32, ph)
            prt = sb("prt1", [P, NB, 3, TW], BF16, ph)
            mean, var = sb("mean0", [P, NB], F32, ph), sb("var0", [P, NB], F32, ph)
            expo = sb("expo0", [P, NB], F32, ph)
            v, ask, answer, tabbed, stored = (sem(n, ph) for n in ("v0", "ask0", "answer0", "tabbed0", "stored0"))
            with nc.Block() as block:
                @block.vector
                def _(e):
                    steps = [0]

                    def done(ins):
                        ins.then_inc(v, 1)
                        steps[0] += 1
                        e.wait_ge(v, steps[0])
                    done(e.memset(expo[:, :], -0.5))
                    done(e.tensor_tensor(tmp[:, :, :], x1[:, :, :], bc_last(dinv[:, :], C), ALU.mult))
                    done(e.tensor_tensor(tmp[:, :, :], tmp[:, :, :], agg[:, :, 0:C], ALU.add))
                    done(e.tensor_tensor(tmp[:, :, :], tmp[:, :, :], bc_last(dinv[:, :], C), ALU.mult))
                    done(e.tensor_tensor(x1[:, :, :], x1[:, :, :], tmp[:, :, :], ALU.add))
                    layer_norm(e, v, steps, x1[:, :, :], tmp[:, :, :], mean, var, expo, [ask, 0, answer])
                    done(e.tensor_copy(tab[:, :, 0:EM], type_e[:, :, EM:2 * EM]))
                    done(e.tensor_tensor(tab[:, :, EM:EM + C], x1[:, :, :], bc_last(nv[:, :], C), ALU.mult))
                    done(e.tensor_copy(tab[:, :, EM + C], nv[:, :]))
                    e.nop().then_inc(tabbed, 1)
                    e.wait_ge(stored, 16)
                    done(e.tensor_copy(prt[:, :, 0, :], tab[:, :, :]))
                    done(e.tensor_tensor(tab[:, :, :], tab[:, :, :], prt[:, :, 0, :], ALU.subtract))
                    done(e.tensor_copy(prt[:, :, 1, :], tab[:, :, :]))
                    done(e.tensor_tensor(prt[:, :, 2, :], tab[:, :, :], prt[:, :, 1, :], ALU.subtract))
                    e.nop().then_inc(tabbed, 1)

                @block.gpsimd
                def _(e):
                    e.wait_ge(ask, 1)
                    e.tensor_tensor(mean[:, :], var[:, :], expo[:, :], ALU.pow).then_inc(answer, 1)

                @block.sync
                def _(e):
                    e.wait_ge(tabbed, 1)
                    e.dma_start(table1.rearrange("(h l) c -> l h c", l=P), tab[:, :, :]).then_inc(stored, 16)
                    e.wait_ge(tabbed, 2)
                    e.dma_start(parts1[0:NN, :].rearrange("(h l) c -> l h c", l=P),
                                prt[:, :, :, :].rearrange("p h k c -> p h (k c)")).then_inc(stored, 16)
                    e.wait_ge(stored, 32)
        agg_ctx.close()

        far_places(1, src_i, "b")
        with ExitStack() as ph:
            ea = sb("ea", [P, SLOTS, G * RA], F32, ph)
            es = sb("es", [P, SLOTS, G * EM], F32, ph)
            win = sb("win", [P, SLOTS, 3 * TW], BF16, ph)
            got = sb("got", [P, SLOTS, G, TW], F32, ph)
            msg = sb("msg", [P, SLOTS, G, RW], F32, ph)
            gidx = sb("gidx1", [P, SLOTS, G], I32, ph)
            sidx = sb("sidx1", [P, SLOTS, G], I32, ph)
            onehot = sb("onehot1", [P, SLOTS, G, P], BF16, ph)
            turned_oh = sb("turned_oh", [P, 2, HG, P], BF16, ph)
            ident16 = sb("ident16b", [P, P], BF16, ph)
            ea_t = sb("ea_t", [2 * RA, 2, 512], F32, ph)
            hid = sb("hid", [2 * C + 1, 2, 512], F32, ph)
            prod = sb("prod", [P, G, EM], F32, ph)
            logit = sb("logit", [P, G], F32, ph)
            val = sb("val", [P, 2, HG, C], F32, ph)
            poh = ps("poh", [P, 2, HG, P], BF16, ph)
            pt = ps("pt", [2 * RA, 512], F32, ph)
            phid = ps("phid", [2 * C, 512], F32, ph)
            gate = ps("gate", [P, 2, 512], F32, ph)
            pwin = ps("pwin", [P, 2, 512], F32, ph)
            gathered = [sem(f"gathered{s}b", ph) for s in range(SLOTS)]
            scattered = [sem(f"scattered{s}b", ph) for s in range(SLOTS)]
            ea_in = [sem(f"ea_in{s}", ph) for s in range(SLOTS)]
            (idx_ready, ones_ready, turned, turned_sb, hidden, hidden_sb, gated, gate_used, msg_ready, own,
             oh_ready, oh_turned, oh_sb, picked, picked_sb) = (
                sem(n + "b", ph) for n in ("idx_ready", "ones_ready", "turned", "turned_sb", "hidden",
                                           "hidden_sb", "gated", "gate_used", "msg_ready", "own", "oh_ready",
                                           "oh_turned", "oh_sb", "picked", "picked_sb"))
            turns_n = NT // SLOTS

            def both_ways(e, program):
                flag = e.value_load(near[0:1, 0:1], min_val=0, max_val=1)
                with e.If(flag == 1):
                    program(True)
                with e.If(flag == 0):
                    program(False)

            def turns(e, tile):
                for s in range(SLOTS):
                    tile(0, s)
                with e.Fori(1, turns_n) as i:
                    for s in range(SLOTS):
                        tile(i, s)

            def halves(i, s, hf):
                return 2 * (SLOTS * i + s) + hf

            def later(i, n, least):
                return not first_turn(i) or n >= least

            with nc.Block() as block:
                @block.sync
                def _(e):
                    def program(is_near):
                        def load(i, s):
                            t = SLOTS * i + s
                            if is_near:
                                first = e.value_load(win_i[0:1, bass.ds(t, 1)], min_val=0, max_val=NN - 1)
                            if not first_turn(i):
                                e.wait_ge(msg_ready, 4 * (t - SLOTS + 1))
                            e.dma_start(ea[:, s, :], edge_attr[bass.ds(t, 1)].rearrange("o p c -> (o p) c")
                                        ).then_inc(ea_in[s], 16)
                            e.dma_start(es[:, s, :], src_emb[:, bass.ds(t * (G * EM), G * EM)]
                                        ).then_inc(ea_in[s], 16)
                            if is_near:
                                e.dma_start(win[:, s, :], parts1[bass.ds(first, P), :]).then_inc(ea_in[s], 16)
                        turns(e, load)
                    both_ways(e, program)

                @block.tensor
                def _(e):
                    e.wait_ge(ones_ready, 2)

                    def program(is_near):
                        def turn_onehots(i, s, hf):
                            n = halves(i, s, hf)
                            if later(i, n, 2):
                                e.wait_ge(oh_sb, n - 1)
                            for g in range(HG):
                                mm = e.transpose(poh[:, hf, g, :], onehot[:, s, hf * HG + g, :], ident16[:, :])
                            mm.then_inc(oh_turned, 1)

                        def turn_attributes(i, s, hf):
                            n = halves(i, s, hf)
                            if later(i, n, 1):
                                e.wait_ge(turned_sb, n)
                            for k in range(4):
                                g = hf * HG + 2 * k
                                mm = e.transpose(pt[:, P * k:P * (k + 1)], ea[:, s, g * RA:(g + 2) * RA],
                                                 ident[:, :])
                            mm.then_inc(turned, 1)

                        def hidden_layer(i, s, hf):
                            n = halves(i, s, hf)
                            e.wait_ge(turned_sb, n + 1)
                            if later(i, n, 1):
                                e.wait_ge(hidden_sb, n)
                            e.matmul(phid[:, :], w1[:, :], ea_t[:, hf, :], start=True,
                                     stop=True).then_inc(hidden, 1)

                        def pick_rows(i, s, hf):
                            n = halves(i, s, hf)
                            e.wait_ge(oh_sb, n + 1)
                            if later(i, n, 1):
                                e.wait_ge(picked_sb, n)
                            for g in range(HG):
                                at = pwin[:, g // 4, TW * (g % 4):TW * (g % 4 + 1)]
                                for k in range(3):
                                    mm = e.matmul(at, turned_oh[:, hf, g, :], win[:, s, TW * k:TW * (k + 1)],
                                                  start=(k == 0), stop=(k == 2))
                            mm.then_inc(picked, 1)

                        def gates(i, s, hf):
                            n = halves(i, s, hf)
                            e.wait_ge(hidden_sb, n + 1)
                            if later(i, n, 2):
                                e.wait_ge(gate_used, n - 1)
                            for k in range(4):
                                mm = e.matmul(gate[:, hf, 2 * C * k:2 * C * (k + 1)],
                                              hid[:, hf, P * k:P * (k + 1)], w2[:, :], start=True, stop=True)
                            mm.then_inc(gated, 1)

                        def tile(i, s):
                            e.wait_ge(ea_in[s], (48 if is_near else 32) * (i + 1))
                            if is_near:
                                e.wait_ge(oh_ready, SLOTS * i + s + 1)
                                turn_onehots(i, s, 0)
                                turn_onehots(i, s, 1)
                            turn_attributes(i, s, 0)
                            hidden_layer(i, s, 0)
                            turn_attributes(i, s, 1)
                            if is_near:
                                pick_rows(i, s, 0)
                            hidden_layer(i, s, 1)
                            gates(i, s, 0)
                            if is_near:
                                pick_rows(i, s, 1)
                            gates(i, s, 1)
                        turns(e, tile)
                    both_ways(e, program)

                @block.scalar
                def _(e):
                    def program(is_near):
                        def copy_onehots(i, s, hf):
                            n = halves(i, s, hf)
                            e.wait_ge(oh_turned, n + 1)
                            if later(i, n, 2):
                                e.wait_ge(picked, n - 1)
                            e.activation(turned_oh[:, hf], poh[:, hf], ACT.Copy).then_inc(oh_sb, 1)

                        def copy_attributes(i, s, hf):
                            n = halves(i, s, hf)
                            e.wait_ge(turned, n + 1)
                            if later(i, n, 2):
                                e.wait_ge(hidden, n - 1)
                            e.activation(ea_t[:, hf, :], pt[:, :], ACT.Copy).then_inc(turned_sb, 1)

                        def silu(i, s, hf):
                            n = halves(i, s, hf)
                            e.wait_ge(hidden, n + 1)
                            if later(i, n, 2):
                                e.wait_ge(gated, n - 1)
                            e.activation(hid[0:2 * C, hf, :], phid[:, :], ACT.Silu,
                                         bias=b1c[:, 0:1]).then_inc(hidden_sb, 1)

                        def copy_rows(i, s, hf):
                            n = halves(i, s, hf)
                            e.wait_ge(picked, n + 1)
                            if not first_turn(i):
                                e.wait_ge(msg_ready, 4 * (SLOTS * (i - 1) + s + 1))
                            rows = pwin[:, :, 0:4 * TW].rearrange("p b (k c) -> p b k c", c=TW)
                            e.activation(got[:, s, hf * HG:(hf + 1) * HG, :].rearrange(
                                "p (b k) c -> p b k c", b=2), rows, ACT.Copy).then_inc(picked_sb, 1)

                        def tile(i, s):
                            if is_near:
                                copy_onehots(i, s, 0)
                            copy_attributes(i, s, 0)
                            if is_near:
                                copy_onehots(i, s, 1)
                            silu(i, s, 0)
                            copy_attributes(i, s, 1)
                            if is_near:
                                copy_rows(i, s, 0)
                            silu(i, s, 1)
                            if is_near:
                                copy_rows(i, s, 1)
                        turns(e, tile)
                    both_ways(e, program)

                @block.vector
                def _(e):
                    e.memset(hid[2 * C:2 * C + 1, :, :], 1.0).then_inc(ones_ready, 1)
                    e.tensor_copy(ident16[:, :], ident[:, :]).then_inc(ones_ready, 1)

                    def program(is_near):
                        def indices(i, s):
                            t = SLOTS * i + s
                            cols = bass.ds(t * G, G)
                            if not first_turn(i):
                                e.wait_ge(scattered[s], 16 * G * i)
                            e.tensor_copy(sidx[:, s, :], pos_i[:, cols]).then_inc(idx_ready, 1)
                            if not is_near:
                                e.tensor_copy(gidx[:, s, :], dst_i[:, cols]).then_inc(idx_ready, 1)

                        def onehots(i, s):
                            t = SLOTS * i + s
                            if not first_turn(i):
                                e.wait_ge(oh_turned, 2 * (t - SLOTS + 1))
                            e.tensor_tensor(onehot[:, s], bc_mid(iota_h[:, :], G),
                                            bc_last(d_off[:, bass.ds(t * G, G)], P),
                                            ALU.is_equal).then_inc(oh_ready, 1)

                        def messages(i, s):
                            t = SLOTS * i + s
                            cols = bass.ds(t * G, G)
                            e.wait_ge(ea_in[s], (48 if is_near else 32) * (i + 1))
                            if is_near:
                                e.wait_ge(picked_sb, 2 * (t + 1))
                            else:
                                e.wait_ge(gathered[s], 16 * G * (i + 1))
                            own0 = 4 * t
                            e.tensor_tensor(prod[:, :, :], es[:, s, :].rearrange("p (g c) -> p g c", c=EM),
                                            got[:, s, :, 0:EM], ALU.mult).then_inc(own, 1)
                            e.wait_ge(own, own0 + 1)
                            e.tensor_reduce(logit[:, :], prod[:, :, :], AX.X, ALU.add).then_inc(own, 1)
                            e.wait_ge(own, own0 + 2)
                            for hf in range(2):
                                gs = slice(hf * HG, (hf + 1) * HG)
                                e.wait_ge(gated, 2 * t + hf + 1)
                                e.tensor_tensor(val[:, hf], gate[:, hf, 0:HG * C].rearrange(
                                    "p (g c) -> p g c", c=C), bc_last(logit[:, gs], C),
                                    ALU.add).then_inc(gate_used, 1)
                            e.wait_ge(gate_used, 2 * t + 2)
                            for hf in range(2):
                                gs = slice(hf * HG, (hf + 1) * HG)
                                e.tensor_tensor(val[:, hf], val[:, hf], got[:, s, gs, EM:EM + C],
                                                ALU.mult).then_inc(own, 1)
                            e.wait_ge(own, own0 + 4)
                            if not first_turn(i):
                                e.wait_ge(scattered[s], 16 * G * i)
                            for hf in range(2):
                                gs = slice(hf * HG, (hf + 1) * HG)
                                e.tensor_tensor(msg[:, s, gs, 0:C], val[:, hf],
                                                bc_last(weight[:, bass.ds(t * G + hf * HG, HG)], C),
                                                ALU.mult).then_inc(msg_ready, 1)
                            e.tensor_copy(msg[:, s, :, C], src_lo[:, cols]).then_inc(msg_ready, 1)
                            e.tensor_copy(msg[:, s, :, C + 1], got[:, s, :, EM + C]).then_inc(msg_ready, 1)
                            e.wait_ge(msg_ready, 4 * t + 2)

                        if is_near:
                            def turn(i, last):
                                for s in range(SLOTS):
                                    if s < SLOTS - 1:
                                        onehots(i, s + 1)
                                    elif not last:
                                        onehots(i + 1, 0)
                                    indices(i, s)
                                    messages(i, s)
                            onehots(0, 0)
                            turn(0, False)
                            with e.Fori(1, turns_n - 1) as i:
                                turn(i, False)
                            turn(turns_n - 1, True)
                            return
                        for s in range(SLOTS):
                            indices(0, s)
                        for s in range(SLOTS):
                            messages(0, s)
                        with e.Fori(1, turns_n) as i:
                            for s in range(SLOTS):
                                indices(i, s)
                            for s in range(SLOTS):
                                messages(i, s)
                    both_ways(e, program)

                @block.gpsimd
                def _(e):
                    e.wait_ge(zeroed, 16 * CLEARS)

                    def program(is_near):
                        def gather(i, s):
                            wait_apart(e, idx_ready, 2 * (SLOTS * i + s + 1), passed)
                            for g in range(G):
                                e.indirect_dma_start(out=got[:, s, g, :], out_offset=None, in_=table1,
                                                     in_offset=bass.IndirectOffsetOnAxis(
                                                         ap=gidx[:, s, g:g + 1], axis=0)
                                                     ).then_inc(gathered[s], 16)

                        def scatter(i, s):
                            t = SLOTS * i + s
                            e.wait_ge(idx_ready, (1 if is_near else 2) * (t + 1))
                            wait_apart(e, msg_ready, 4 * (t + 1), passed)
                            for g in range(G):
                                e.indirect_dma_start(out=perm1,
                                                     out_offset=bass.IndirectOffsetOnAxis(
                                                         ap=sidx[:, s, g:g + 1], axis=0),
                                                     in_=msg[:, s, g, :], in_offset=None
                                                     ).then_inc(scattered[s], 16)
                        if is_near:
                            turns(e, scatter)
                        else:
                            for s in range(SLOTS):
                                gather(0, s)
                            for s in range(SLOTS):
                                scatter(0, s)
                            with e.Fori(1, turns_n) as i:
                                for s in range(SLOTS):
                                    gather(i, s)
                                for s in range(SLOTS):
                                    scatter(i, s)
                        for s in range(SLOTS):
                            e.wait_ge(scattered[s], 16 * G * turns_n)
                    both_ways(e, program)

        with ExitStack() as ph:
            agg = sb("agg1", [P, NB, RW], F32, ph)
            reduce_rows(1, perm1, agg, "b", False)
            tmp = sb("tmp1", [P, NB, C], F32, ph)
            y = sb("y1", [P, NB, C], F32, ph)
            mean, var = sb("mean1", [P, NB], F32, ph), sb("var1", [P, NB], F32, ph)
            expo = sb("expo1", [P, NB], F32, ph)
            v, ask, answer, ready, stored = (sem(n, ph) for n in ("v1", "ask1", "answer1", "ready1", "stored1"))
            with nc.Block() as block:
                @block.vector
                def _(e):
                    steps = [0]

                    def done(ins):
                        ins.then_inc(v, 1)
                        steps[0] += 1
                        e.wait_ge(v, steps[0])
                    power = [ask, 0, answer]
                    done(e.memset(expo[:, :], -0.5))
                    done(e.tensor_scalar(var[:, :], agg[:, :, C + 1], 1e-8, None, ALU.max))
                    done(e.reciprocal(mean[:, :], var[:, :]))
                    done(e.tensor_tensor(y[:, :, :], agg[:, :, 0:C], bc_last(mean[:, :], C), ALU.mult))
                    done(e.tensor_tensor(y[:, :, :], y[:, :, :], x1[:, :, :], ALU.add))
                    layer_norm(e, v, steps, y[:, :, :], tmp[:, :, :], mean, var, expo, power)
                    done(e.tensor_tensor(y[:, :, :], y[:, :, :], bc_mid(gam[:, :], NB), ALU.mult))
                    done(e.tensor_tensor(y[:, :, :], y[:, :, :], bc_mid(bet[:, :], NB), ALU.add))
                    done(e.tensor_tensor(y[:, :, :], y[:, :, :], x1[:, :, :], ALU.add))
                    layer_norm(e, v, steps, y[:, :, :], tmp[:, :, :], mean, var, expo, power)
                    e.nop().then_inc(ready, 1)

                @block.gpsimd
                def _(e):
                    for k in range(2):
                        e.wait_ge(ask, k + 1)
                        e.tensor_tensor(mean[:, :], var[:, :], expo[:, :], ALU.pow).then_inc(answer, 1)

                @block.sync
                def _(e):
                    e.wait_ge(ready, 1)
                    full = NODES // P
                    e.dma_start(out[0:full * P, :].rearrange("(h l) c -> l h c", l=P),
                                y[:, 0:full, :]).then_inc(stored, 16)
                    e.dma_start(out[full * P:NODES, :], y[0:NODES - full * P, full, :]).then_inc(stored, 16)
                    e.wait_ge(stored, 32)


def kernel(**inputs):
    import numpy as np
    import concourse.bacc as bacc
    from concourse.bass_utils import run_bass_kernel_spmd

    a = {k: np.ascontiguousarray(v) for k, v in inputs.items()}

    def padded(v, n, fill=0):
        out = np.full((n,) + v.shape[1:], fill, v.dtype)
        out[:v.shape[0]] = v
        return out

    def by_tile(v, fill=0):
        return np.ascontiguousarray(padded(v, K * P, fill).reshape(NT, P, G).transpose(1, 0, 2).reshape(P, K))

    def by_node(v):
        return np.ascontiguousarray(padded(v, NN).reshape(NB, P).T)

    f = {
        "x": padded(a["x"], NN),
        "src": by_tile(a["src"], NN - 1),
        "dst": by_tile(a["dst"], NN - 1),
        "edge_attr": padded(a["edge_attr_40"], K * P).reshape(NT, P, G * RA),
        "edge_weight": by_tile(a["edge_weight"]),
        "node_type": by_node(a["node_type_119"]),
        "node_vec": by_node(a["node_vec"]),
        "W1T": np.ascontiguousarray(a["L1_gnn_W1"].T),
        "b1": a["L1_gnn_b1"].reshape(C, 1),
        "W2T": np.ascontiguousarray(a["L1_gnn_W2"].T),
        "b2": a["L1_gnn_b2"].reshape(1, C),
        "emb": a["L1_gnn_emb"],
        "embT": np.ascontiguousarray(a["L1_gnn_emb"].T),
        "adaptWT": np.ascontiguousarray(a["L1_gnn_adaptW"].T),
        "gamma": a["L1_gnn_gamma"].reshape(1, C),
        "beta": a["L1_gnn_beta"].reshape(1, C),
    }
    nc = bacc.Bacc("TRN2", target_bir_lowering=False, num_devices=1)
    args = {k: nc.dram_tensor("in_" + k, v.shape, mybir.dt.from_np(v.dtype), kind="ExternalInput").ap()
            for k, v in f.items()}
    out = nc.dram_tensor("out_nodes", (NODES, C), F32, kind="ExternalOutput").ap()
    build(nc, out=out, **args)
    r = run_bass_kernel_spmd(nc, [{"in_" + k: v for k, v in f.items()}], core_ids=[0])
    return r.results[0]["out_nodes"]
```

```python
from contextlib import ExitStack, contextmanager

import concourse.bass as bass
from concourse import mybir

F32 = mybir.dt.float32
BF16 = mybir.dt.bfloat16
I32 = mybir.dt.int32
U16 = mybir.dt.uint16
ALU = mybir.AluOpType
ACT = mybir.ActivationFunctionType
AX = mybir.AxisListType

P = 128
NODES = 6250
EDGES = 206250
C = 48
RA = 40
EM = 32
NEL = 119
CUTOFF = 6.0
EPS = 1e-5

NB = -(-NODES // P)
NN = NB * P
G = 16
SLOTS = 3
NT = -(-EDGES // (P * G))
K = NT * G
RW = C + 2
RG = 16
RS = 8
ROH = RS // 2
U = 2
RT = -(-(K + U * NB) // RG)
RT += RT % 2
RC = RT * RG
RCP = -(-RC // (U * P))
AW = 64
HG = G // 2
TW = EM + C + 1
PW = -(-3 * TW // 256) * 256
PB = 2
SW = PB * (NT // SLOTS - 1)
TAIL = RT - NT


def log2(n):
    assert n & (n - 1) == 0
    return n.bit_length() - 1


def bc_mid(ap, n):
    return ap.unsqueeze(1).broadcast_to([ap.shape[0], n, ap.shape[1]])


def bc_last(ap, n):
    return ap.unsqueeze(2).broadcast_to([ap.shape[0], ap.shape[1], n])


def wait_apart(e, sem, value, passed):
    e.wait_ge(sem, value)
    e.sem_inc(passed, 1)


def first_turn(i):
    return isinstance(i, int) and i == 0


def over_tiles(e, n, slots, *steps, beside=None, after={}):
    assert all(lag <= n % slots for _, lag in steps)
    for t in range(slots + n % slots):
        for step, lag in steps:
            if t >= lag:
                step(*divmod(t - lag, slots))
        if t in after:
            after[t]()
    with e.Fori(1, n // slots) as turn:
        for k in range(slots):
            for step, lag in steps:
                ahead, s = divmod(n % slots + k - lag, slots)
                step(turn + ahead if ahead else turn, s)
        if beside:
            beside(turn)
    if n - 1 in after:
        after[n - 1]()
    for t in range(n, n + max(lag for _, lag in steps)):
        for step, lag in steps:
            if t - lag < n:
                step(*divmod(t - lag, slots))


def tiles_of(s, n, slots):
    return (n - s + slots - 1) // slots


def build(nc, x, src, dst, edge_attr, edge_weight, node_type, node_vec, W1T, b1, W2T, b2,
          emb, embT, adaptWT, gamma, beta, out):
    table0 = nc.dram_tensor("table0", (NN, EM + C), F32).ap()
    table1 = nc.dram_tensor("table1", (NN, TW), F32).ap()
    parts1 = nc.dram_tensor("parts1", (NN + P, PW), BF16).ap()
    type_rows = nc.dram_tensor("type_rows", (NEL, 2 * EM), F32).ap()
    src_emb = nc.dram_tensor("src_emb", (P, K * EM), F32).ap()
    perm0 = nc.dram_tensor("perm0", (RC * P, RW), F32).ap()
    perm1 = nc.dram_tensor("perm1", (RC * P, RW), F32).ap()
    bucket_of = nc.dram_tensor("bucket_of", (2, P * RCP), I32).ap()

    ctx = ExitStack()
    with ctx:
        def sb(name, shape, dt=F32, to=ctx):
            return to.enter_context(nc.sbuf_tensor(name, shape, dt))

        def ps(name, shape, dt=F32, to=ctx):
            return to.enter_context(nc.psum_tensor(name, shape, dt))

        def sem(name, to=ctx):
            return to.enter_context(nc.semaphore(name))

        passed = sem("passed")
        iota_f = sb("iota_f", [P, P])
        iota_p = sb("iota_p", [P, 1])
        ident = sb("ident", [P, P])
        below = sb("below", [P, P])
        ones = sb("ones", [P, P])
        number = sb("number", [P, P, G], BF16)
        ident16 = sb("ident16", [P, P], BF16)
        zero16 = sb("zero16", [P, 512], BF16)
        src_i = sb("src_i", [P, K], I32)
        dst_i = sb("dst_i", [P, K], I32)
        pos_i = sb("pos_i", [P, K], I32)
        start = sb("start", [P, SW])
        win_f = sb("win_f", [P, NT])
        win_i = sb("win_i", [P, NT], I32)
        near = sb("near", [P, 1], I32)
        d_off = sb("d_off", [P, K], BF16)
        src_lo = sb("src_lo", [P, K])
        weight = sb("weight", [P, K])
        nv = sb("nv", [P, NB])
        dinv = sb("dinv", [P, NB])
        type_e = sb("type_e", [P, NB, 2 * EM])
        x1 = sb("x1", [P, NB, C])
        z_i = sb("z_i", [P, NB], I32)
        src_cnt = sb("src_cnt", [P, NB])
        far_cnt = sb("far_cnt", [P, NB])
        w1 = sb("w1", [2 * RA, 2 * C])
        w2 = sb("w2", [2 * C + 1, 2 * C])
        b1c = sb("b1c", [2 * C, 1])
        gam = sb("gam", [P, C])
        bet = sb("bet", [P, C])

        zeros = sb("zeros", [P, RG * RW])

        PART = -(-NB // 4)
        PARTS = [(a, min(a + PART, NB)) for a in range(0, NB, PART)]

        def in_waves(*stages):
            for wave in range(len(PARTS) + len(stages) - 1):
                for j, stage in enumerate(stages):
                    if stage and 0 <= wave - j < len(PARTS):
                        stage(wave - j, *PARTS[wave - j])

        with ExitStack() as ph:
            embt = sb("embt", [EM, NEL], F32, ph)
            adt = sb("adt", [EM, EM], F32, ph)
            trow = sb("trow", [NEL, 2 * EM], F32, ph)
            hi_i = sb("hi_i", [P, K], I32, ph)
            lo_i = sb("lo_i", [P, K], I32, ph)
            lo16 = sb("lo16", [P, K], BF16, ph)
            hi16 = sb("hi16", [P, K], BF16, ph)
            oh_lo = sb("oh_lo", [P, 2, P, G], BF16, ph)
            oh_hi = sb("oh_hi", [P, 2, NB, G], BF16, ph)
            tab = sb("tab", [P, NB, EM + C], F32, ph)
            expo = sb("expo", [P, NB], F32, ph)
            deg1 = sb("deg1", [P, NB], F32, ph)
            dst_f = sb("dst_f", [P, K], F32, ph)
            low, high = sb("low", [P, NT], F32, ph), sb("high", [P, NT], F32, ph)
            ends2 = sb("ends2", [P, 2], F32, ph)
            diag = sb("diag", [P, 2, NT], F32, ph)
            worst = sb("worst", [P, 1], F32, ph)
            qps = ps("qps", [NEL, EM], F32, ph)
            deg = ps("deg", [P, 512], F32, ph)
            cntp = ps("cntp", [P, 512], F32, ph)
            turned = ps("turned_w", [P, 2, 512], F32, ph)
            spread_w = ps("spread_w", [P, 2, 512], F32, ph)
            (src_in, dst_in, wl, types_in, tready, tstored, types_got, qready, wz, io, blank, consts, keyed,
             oh_ready, oh_used, counted, degs, roots, tabbed, stored, v, across, spread_done) = (
                sem(n, ph) for n in ("src_in", "dst_in", "wl", "types_in", "tready", "tstored", "types_got",
                                     "qready", "wz", "io", "blank", "consts", "keyed", "oh_ready", "oh_used",
                                     "counted", "degs", "roots", "tabbed", "stored", "v_w", "across_w",
                                     "spread_done_w"))
            with nc.Block() as block:
                @block.sync
                def _(e):
                    e.dma_start(src_i[:, :], src).then_inc(src_in, 16)
                    e.dma_start(dst_i[:, :], dst).then_inc(dst_in, 16)
                    e.dma_start(weight[:, :], edge_weight).then_inc(wl, 16)
                    e.dma_start(x1[:, :, :], x.rearrange("(h l) c -> l h c", l=P)).then_inc(wl, 16)
                    e.dma_start(nv[:, :], node_vec).then_inc(wl, 16)
                    e.dma_start(b1c[0:C, :], b1).then_inc(wl, 16)
                    e.dma_start(b1c[C:2 * C, :], b1).then_inc(wl, 16)
                    e.dma_start(gam[:, :], gamma.broadcast_to([P, C])).then_inc(wl, 16)
                    e.dma_start(bet[:, :], beta.broadcast_to([P, C])).then_inc(wl, 16)
                    e.wait_ge(wz, 2)
                    for k in range(2):
                        e.dma_start(w1[RA * k:RA * (k + 1), C * k:C * (k + 1)], W1T).then_inc(wl, 16)
                        e.dma_start(w2[C * k:C * (k + 1), C * k:C * (k + 1)], W2T).then_inc(wl, 16)
                        e.dma_start(w2[2 * C:2 * C + 1, C * k:C * (k + 1)], b2).then_inc(wl, 16)
                    e.wait_ge(blank, 1)
                    e.dma_start(parts1[NN:NN + P, :], zeros[:, 0:PW // 2].bitcast(BF16)
                                ).then_inc(wl, 16)
                    e.wait_ge(wl, 16 * 14)
                    for k, (a, b) in enumerate(PARTS):
                        e.wait_ge(tabbed, k + 1)
                        e.dma_start(table0[P * a:P * b, :].rearrange("(h l) c -> l h c", l=P),
                                    tab[:, a:b, :]).then_inc(stored, 16)
                    e.wait_ge(stored, 16 * len(PARTS))

                @block.scalar
                def _(e):
                    e.dma_start(z_i[:, :], node_type).then_inc(types_in, 16)
                    e.dma_start(embt[:, :], embT).then_inc(types_in, 16)
                    e.dma_start(adt[:, :], adaptWT).then_inc(types_in, 16)
                    e.dma_start(trow[:, 0:EM], emb).then_inc(types_in, 16)
                    e.wait_ge(qready, 1)
                    e.activation(trow[:, EM:2 * EM], qps[:, :], ACT.Copy).then_inc(tready, 1)
                    e.wait_ge(types_in, 64)
                    e.wait_ge(tready, 1)
                    e.dma_start(type_rows, trow[:, :]).then_inc(tstored, 16)
                    e.wait_ge(types_got, 16 * NB)
                    e.activation(tab[:, :, 0:EM], type_e[:, :, 0:EM], ACT.Copy).then_inc(tready, 1)

                @block.tensor
                def _(e):
                    e.wait_ge(keyed, 3)
                    e.matmul(cntp[:, :], zero16[:, 0:P], zero16[:, :], start=True, stop=False,
                             skip_group_check=True)
                    e.matmul(deg[:, :], zero16[:, 0:P], zero16[:, :], start=True, stop=False,
                             skip_group_check=True).then_inc(oh_used, 2)
                    e.wait_ge(types_in, 64)
                    e.matmul(qps[:, :], embt[:, :], adt[:, :], start=True, stop=True).then_inc(qready, 1)

                    def count(i, s):
                        e.wait_ge(oh_ready, 2 * (2 * i + s + 1))
                        for g in range(G):
                            e.matmul(cntp[:, 0:NB], ident16[:, :], oh_hi[:, s, :, g],
                                     start=False, stop=False, skip_group_check=True)
                            mm = e.matmul(deg[:, 0:NB], oh_lo[:, s, :, g], oh_hi[:, s, :, g],
                                          start=False, stop=False, skip_group_check=True)
                        mm.then_inc(oh_used, 1)
                    over_tiles(e, NT, 2, (count, 0))
                    e.matmul(cntp[:, :], zero16[:, 0:P], zero16[:, :], start=False, stop=True,
                             skip_group_check=True)
                    e.matmul(deg[:, :], zero16[:, 0:P], zero16[:, :], start=False, stop=True,
                             skip_group_check=True).then_inc(counted, 1)
                    e.wait_ge(v, 3)
                    e.transpose(turned[0:NT, 0, 0:P], low[:, :], ident[:, :]).then_inc(across, 1)
                    e.transpose(turned[0:NT, 1, 0:P], high[:, :], ident[:, :]).then_inc(across, 1)
                    e.wait_ge(v, 8)
                    for k in range(2):
                        e.matmul(spread_w[:, k, 0:NT], ones[0:NT, :], diag[0:NT, k, :], start=True,
                                 stop=True).then_inc(spread_done, 1)

                @block.gpsimd
                def _(e):
                    e.iota(iota_f[:, :], [[1, P]], base=0, channel_multiplier=0,
                           allow_small_or_imprecise_dtypes=True).then_inc(io, 1)
                    e.iota(iota_p[:, :], [[0, 1]], base=0, channel_multiplier=1,
                           allow_small_or_imprecise_dtypes=True).then_inc(io, 1)
                    e.memset(zeros[:, :], 0.0).then_inc(blank, 1)
                    e.wait_ge(types_in, 64)
                    e.wait_ge(tstored, 16)
                    for h in range(NB):
                        e.indirect_dma_start(out=type_e[:, h, :], out_offset=None, in_=type_rows,
                                             in_offset=bass.IndirectOffsetOnAxis(ap=z_i[:, h:h + 1], axis=0)
                                             ).then_inc(types_got, 16)
                    e.wait_ge(types_got, 16 * NB)
                    e.wait_ge(degs, 1)
                    for a, b in PARTS:
                        e.tensor_tensor(dinv[:, a:b], deg1[:, a:b], expo[:, a:b], ALU.pow).then_inc(roots, 1)

                @block.vector
                def _(e):
                    steps = [0]

                    def done(ins):
                        ins.then_inc(v, 1)
                        steps[0] += 1
                        e.wait_ge(v, steps[0])
                    e.memset(w1[:, :], 0.0).then_inc(wz, 1)
                    e.memset(w2[:, :], 0.0).then_inc(wz, 1)
                    e.memset(zero16[:, :], 0.0)
                    e.memset(expo[:, :], -0.5)
                    e.wait_ge(io, 2)
                    e.tensor_scalar(ident[:, :], iota_f[:, :], iota_p[:, 0:1], None, ALU.is_equal
                                    ).then_inc(keyed, 1)
                    e.tensor_copy(number[:, :, :], bc_last(iota_f[:, :], G)).then_inc(keyed, 1)
                    e.wait_ge(keyed, 2)
                    e.tensor_copy(ident16[:, :], ident[:, :]).then_inc(keyed, 1)
                    e.wait_ge(src_in, 16)
                    e.tensor_scalar(hi_i[:, :], src_i[:, :], 7, None, ALU.logical_shift_right).then_inc(consts, 1)
                    e.tensor_scalar(lo_i[:, :], src_i[:, :], P - 1, None, ALU.bitwise_and).then_inc(consts, 1)
                    e.wait_ge(consts, 2)
                    e.tensor_copy(hi16[:, :], hi_i[:, :]).then_inc(consts, 1)
                    e.tensor_copy(lo16[:, :], lo_i[:, :]).then_inc(consts, 1)
                    e.wait_ge(consts, 4)

                    def onehots(i, s):
                        t = 2 * i + s
                        e.wait_ge(oh_used, t + 1)
                        e.tensor_tensor(oh_lo[:, s], number[:, :, :], bc_mid(lo16[:, bass.ds(t * G, G)], P),
                                        ALU.is_equal).then_inc(oh_ready, 1)
                        e.tensor_tensor(oh_hi[:, s], number[:, 0:NB, :],
                                        bc_mid(hi16[:, bass.ds(t * G, G)], NB),
                                        ALU.is_equal).then_inc(oh_ready, 1)
                    over_tiles(e, NT, 2, (onehots, 0))
                    by_tile = dst_f[:, :].rearrange("p (t g) -> p t g", g=G)
                    e.wait_ge(dst_in, 16)
                    done(e.tensor_copy(dst_f[:, :], dst_i[:, :]))
                    e.wait_ge(counted, 1)
                    e.tensor_scalar(deg1[:, :], deg[:, 0:NB], 1.0, None, ALU.add).then_inc(degs, 1)
                    e.memset(ones[:, :], 1.0)
                    done(e.tensor_reduce(low[:, :], by_tile, AX.X, ALU.min))
                    done(e.tensor_reduce(high[:, :], by_tile, AX.X, ALU.max))
                    e.wait_ge(wl, 16 * 14)
                    e.wait_ge(tready, 2)
                    for k, (a, b) in enumerate(PARTS):
                        e.wait_ge(roots, k + 1)
                        e.tensor_tensor(tab[:, a:b, EM:EM + C], x1[:, a:b, :], bc_last(dinv[:, a:b], C),
                                        ALU.mult).then_inc(tabbed, 1)
                    e.tensor_scalar(below[:, :], iota_f[:, :], iota_p[:, 0:1], None, ALU.is_gt)
                    e.tensor_copy(src_cnt[:, :], cntp[:, 0:NB])
                    e.tensor_copy(src_lo[:, :], lo_i[:, :])
                    e.wait_ge(across, 2)
                    done(e.tensor_reduce(ends2[0:NT, 0:1], turned[0:NT, 0, 0:P], AX.X, ALU.min))
                    done(e.tensor_reduce(ends2[0:NT, 1:2], turned[0:NT, 1, 0:P], AX.X, ALU.max))
                    done(e.tensor_tensor(ends2[0:NT, 1:2], ends2[0:NT, 1:2], ends2[0:NT, 0:1], ALU.subtract))
                    for k in range(2):
                        done(e.tensor_scalar(diag[0:NT, k, :], ident[0:NT, 0:NT], ends2[0:NT, k:k + 1], None,
                                             ALU.mult))
                    e.wait_ge(spread_done, 2)
                    done(e.tensor_copy(win_f[:, :], spread_w[:, 0, 0:NT]))
                    done(e.tensor_copy(win_i[:, :], win_f[:, :]))
                    done(e.tensor_reduce(worst[:, :], spread_w[:, 1, 0:NT], AX.X, ALU.max))
                    done(e.tensor_scalar(near[:, :], worst[:, :], float(P), None, ALU.is_lt))
                    done(e.tensor_tensor(d_off[:, :].rearrange("p (t g) -> p t g", g=G), by_tile,
                                         bc_last(win_f[:, :], G), ALU.subtract))

        @contextmanager
        def only(e, general):
            if not general:
                yield
                return
            flag = e.value_load(near[0:1, 0:1], min_val=0, max_val=1)
            with e.If(flag == 0):
                yield

        class Starts:

            def __init__(self, which, count, perm, tag, ph):
                self.which, self.count, self.perm = which, count, perm
                self.last_f = sb("last_f" + tag, [P, NB], F32, ph)
                self.last_i = sb("last_i" + tag, [P, 2, NB], I32, ph)
                self.last_row = sb("last_row" + tag, [P, SW], I32, ph)
                self.tot_i = sb("tot_i" + tag, [P, NB], I32, ph)
                self.units = sb("units" + tag, [P, NB], F32, ph)
                self.ends = sb("ends" + tag, [P, NB], F32, ph)
                self.cid = sb("cid" + tag, [P, RCP], F32, ph)
                self.cmp = sb("cmp" + tag, [P, RCP, NB], F32, ph)
                self.bof = sb("bof" + tag, [P, RCP], F32, ph)
                self.bof_i = sb("bof_i" + tag, [P, RCP], I32, ph)
                self.pref = ps("pref" + tag, [P, 2, 512], F32, ph)
                self.v, self.summed, self.cid_in, self.bst, self.cleared = (
                    sem(n + tag, ph) for n in ("vs", "summed", "cid_in", "bst", "cleared"))

            def pool(self, e):
                e.iota(self.cid[:, :], [[1, RCP]], base=0, channel_multiplier=RCP,
                       allow_small_or_imprecise_dtypes=True).then_inc(self.cid_in, 1)

            def tensor(self, e):
                for k, by in enumerate((below, ones)):
                    e.matmul(self.pref[:, k, 0:NB], by[:, :], self.count[:, :], start=True,
                             stop=True).then_inc(self.summed, 1)

            def clear_tail(self, e):
                tail = self.perm[NT * G * P:RC * P, :].rearrange("(t p g) c -> t p (g c)", p=P, g=RG)
                for t in range(TAIL):
                    e.dma_start(tail[t], zeros[:, :]).then_inc(self.cleared, 16)

            def clear_last(self, e, h):
                e.wait_ge(self.v, self.STEPS)
                e.wait_ge(self.cleared, 16 * (TAIL + h))
                first = e.value_load(self.last_row[0:1, bass.ds(h, 1)], min_val=0,
                                     max_val=((RC - RG) * P + RG) // U - 1)
                e.dma_start(self.perm.rearrange("(q u) c -> q (u c)", u=U)[bass.ds(first, P, RG // U), :],
                            zeros[:, 0:U * RW]).then_inc(self.cleared, 16)

            def store(self, e, buckets):
                e.wait_ge(self.v, self.STEPS)
                e.dma_start(bucket_of[self.which:self.which + 1, :].rearrange("o (p q) -> (o p) q", q=RCP),
                            self.bof_i[:, :]).then_inc(self.bst, 16)
                e.wait_ge(self.bst, 16)
                e.wait_ge(self.cleared, 16 * (TAIL + buckets))

            STEPS = 18

            def vector(self, e):
                tot_i, units, ends, cid, cmp = self.tot_i, self.units, self.ends, self.cid, self.cmp
                bof, bof_i, pref = self.bof, self.bof_i, self.pref
                steps = [0]

                def done(ins):
                    ins.then_inc(self.v, 1)
                    steps[0] += 1
                    e.wait_ge(self.v, steps[0])
                done(e.memset(start[:, NB:SW], 0.0))
                e.wait_ge(self.summed, 2)
                done(e.tensor_scalar(tot_i[:, :], pref[:, 1, 0:NB], float(U * P - 1), None, ALU.add))
                done(e.tensor_scalar(tot_i[:, :], tot_i[:, :], log2(U * P), None, ALU.logical_shift_right))
                done(e.tensor_copy(units[:, :], tot_i[:, :]))
                done(e.tensor_tensor_scan(ends[:, :], units[:, :], units[:, :], 0.0, ALU.add,
                                          ALU.bypass))
                done(e.tensor_tensor(start[:, 0:NB], ends[:, :], units[:, :], ALU.subtract))
                done(e.tensor_scalar(start[:, 0:NB], start[:, 0:NB], float(U * P), -1.0, ALU.mult,
                                     ALU.add))
                e.wait_ge(self.cid_in, 1)
                done(e.tensor_tensor(cmp[:, :, :], bc_last(cid[:, :], NB), bc_mid(ends[:, :], RCP), ALU.is_ge))
                done(e.tensor_reduce(bof[:, :], cmp[:, :, :], AX.X, ALU.add))
                done(e.tensor_scalar(bof[:, :], bof[:, :], float(NB - 1), float(AW), ALU.min, ALU.mult))
                done(e.tensor_copy(bof_i[:, :], bof[:, :]))
                done(e.tensor_tensor(start[:, 0:NB], start[:, 0:NB], pref[:, 0, 0:NB], ALU.add))
                last_f, last_i, last_row = self.last_f, self.last_i, self.last_row
                done(e.memset(last_row[:, NB:SW], 0))
                done(e.tensor_scalar(last_f[:, :], ends[:, :], -1.0, 0.0, ALU.add, ALU.max))
                done(e.tensor_copy(last_i[:, 0, :], last_f[:, :]))
                done(e.tensor_scalar(last_i[:, 1, :], last_i[:, 0, :], RG // U - 1, None, ALU.bitwise_and))
                done(e.tensor_scalar(last_i[:, 0, :], last_i[:, 0, :], log2(RG // U), log2(P * RG // U),
                                     ALU.logical_shift_right, ALU.logical_shift_left))
                done(e.tensor_tensor(last_row[:, 0:NB], last_i[:, 0, :], last_i[:, 1, :], ALU.bitwise_or))
                assert steps[0] == self.STEPS

        def place_bucket(e, h, tiles, done):
            key, mask, run, pos = tiles
            done(e.tensor_scalar(mask[:, :], key[:, :], iota_f[:, bass.ds(h, 1)], None, ALU.is_equal))
            done(e.tensor_tensor_scan(run[:, :], mask[:, :], mask[:, :], start[:, bass.ds(h, 1)], ALU.add,
                                      ALU.bypass))
            done(e.copy_predicated(pos[:, :], mask[:, :], run[:, :]))

        def rows_of_places(e, pos, a, b, done):
            done(e.tensor_copy(a[:, :], pos[:, :]))
            done(e.tensor_scalar(b[:, :], a[:, :], P - 1, 4, ALU.bitwise_and, ALU.logical_shift_left))
            done(e.tensor_scalar(pos_i[:, :], a[:, :], 7, RG - 1, ALU.logical_shift_right, ALU.bitwise_and))
            done(e.tensor_tensor(pos_i[:, :], pos_i[:, :], b[:, :], ALU.bitwise_or))
            done(e.tensor_scalar(a[:, :], a[:, :], 11, 11, ALU.logical_shift_right, ALU.logical_shift_left))
            done(e.tensor_tensor(pos_i[:, :], pos_i[:, :], a[:, :], ALU.bitwise_or))

        def far_places(which, node, perm, tag):
            with ExitStack() as ph:
                key = sb("key" + tag, [P, K], F32, ph)
                key_i = sb("key_i" + tag, [P, K], I32, ph)
                mask = sb("mask" + tag, [P, K], U16, ph)
                run = sb("run" + tag, [P, K], F32, ph)
                pos = sb("pos" + tag, [P, K], F32, ph)
                v, turn, counts = (sem(n + tag, ph) for n in ("v", "turn", "counts"))
                starts = Starts(which, far_cnt, perm, tag, ph)
                with nc.Block() as block:
                    @block.vector
                    def _(e):
                        steps = [0]

                        def done(ins):
                            ins.then_inc(v, 1)
                            steps[0] += 1
                            e.wait_ge(v, steps[0])
                        with only(e, True):
                            done(e.tensor_scalar(key_i[:, :], node[:, :], 7, None, ALU.logical_shift_right))
                            done(e.tensor_copy(key[:, :], key_i[:, :]))
                            for h in range(NB):
                                done(e.tensor_scalar(run[:, :], key[:, :], float(h), 0.0, ALU.is_equal,
                                                     ALU.add, accum_out=far_cnt[:, h:h + 1]))
                            e.nop().then_inc(counts, 1)
                            starts.vector(e)
                            done(e.memset(pos[:, :], 0.0))
                            with e.Fori(0, NB) as h:
                                own = [0]

                                def in_turn(ins):
                                    ins.then_inc(turn, 1)
                                    own[0] += 1
                                    e.wait_ge(turn, 3 * h + own[0])
                                    e.sem_inc(passed, 1)
                                place_bucket(e, h, (key, mask, run, pos), in_turn)
                            rows_of_places(e, pos, key_i, run[:, :].bitcast(I32), done)

                    @block.gpsimd
                    def _(e):
                        starts.pool(e)

                    @block.tensor
                    def _(e):
                        with only(e, True):
                            e.wait_ge(counts, 1)
                            starts.tensor(e)

                    @block.sync
                    def _(e):
                        with only(e, True):
                            starts.clear_tail(e)
                            with e.Fori(0, NB) as h:
                                starts.clear_last(e, h)
                            starts.store(e, NB)

        def reduce_rows(which, perm, result, tag, general):
            with ExitStack() as ph:
                acc = ps("acc" + tag, [P, 7, 512], F32, ph)
                rows = sb("rows" + tag, [P, RS, RG, RW], F32, ph)
                part = sb("part" + tag, [P, RS, 3, RG, RW], BF16, ph)
                onehot = sb("onehot" + tag, [P, ROH, P, RG], BF16, ph)
                low16 = sb("low16" + tag, [P, RS, RG], BF16, ph)
                btab = sb("btab" + tag, [1, P * RCP], I32, ph)
                rows_in = [sem(f"rows_in{s}" + tag, ph) for s in range(RS)]
                keyed, bt_in, oh_ready, used, high, rested, mid, lowp, summed = (
                    sem(n + tag, ph) for n in ("keyed_r", "bt_in", "oh_ready_r", "used", "high", "rested", "mid",
                                               "lowp", "summed_r"))
                rows_d = perm.rearrange("(t p g) c -> t p (g c)", p=P, g=RG)

                def freed(e, i, s):
                    if not first_turn(i):
                        e.wait_ge(used, RS * (i - 1) + s + 1)

                with nc.Block() as block:
                    @block.sync
                    def _(e):
                        def load(i, s):
                            freed(e, i, s)
                            e.dma_start(rows[:, s].rearrange("p g c -> p (g c)"),
                                        rows_d[bass.ds(RS * i + s, 1)].rearrange("o p c -> (o p) c")
                                        ).then_inc(rows_in[s], 16)
                        with only(e, general):
                            e.dma_start(btab[:, :], bucket_of[which:which + 1, :]).then_inc(bt_in, 16)
                            over_tiles(e, RT, RS, (load, 0))
                            e.wait_ge(summed, 1)

                    @block.scalar
                    def _(e):
                        def high_part(i, s):
                            e.wait_ge(rows_in[s], 16 * (i + 1))
                            freed(e, i, s)
                            e.activation(low16[:, s, :], rows[:, s, :, C], ACT.Copy).then_inc(keyed, 1)
                            e.activation(part[:, s, 0], rows[:, s], ACT.Copy).then_inc(high, 1)

                        def middle_part(i, s):
                            e.wait_ge(rested, RS * i + s + 1)
                            e.activation(part[:, s, 1], rows[:, s], ACT.Copy).then_inc(mid, 1)
                        with only(e, general):
                            over_tiles(e, RT, RS, (high_part, 0), (middle_part, 1))

                    @block.gpsimd
                    def _(e):
                        def take(i, s):
                            e.wait_ge(high, RS * i + s + 1)
                            e.tensor_tensor(rows[:, s], rows[:, s], part[:, s, 0],
                                            ALU.subtract).then_inc(rested, 1)
                        with only(e, general):
                            over_tiles(e, RT, RS, (take, 0))

                    @block.vector
                    def _(e):
                        def onehots(i, s):
                            e.wait_ge(keyed, RS * i + s + 1)
                            if not first_turn(i) or s >= ROH:
                                e.wait_ge(used, RS * i + s - ROH + 1)
                            e.tensor_tensor(onehot[:, s % ROH], number[:, :, :], bc_mid(low16[:, s, :], P),
                                            ALU.is_equal).then_inc(oh_ready, 1)

                        def low_part(i, s):
                            e.wait_ge(mid, RS * i + s + 1)
                            e.tensor_tensor(part[:, s, 2], rows[:, s], part[:, s, 1],
                                            ALU.subtract).then_inc(lowp, 1)
                        with only(e, general):
                            over_tiles(e, RT, RS, (onehots, 1), (low_part, 2))
                            e.wait_ge(summed, 1)
                            e.tensor_copy(result[:, 0:48, :], acc[:, 0:6, :].rearrange(
                                "p b (k c) -> p (b k) c", c=AW)[:, :, 0:RW])
                            e.tensor_copy(result[:, 48:NB, :], acc[:, 6:7, 0:AW][:, :, 0:RW])

                    @block.tensor
                    def _(e):
                        regs = [e.alloc_register(f"bucket{g}" + tag) for g in range(2 * RG // U)]
                        flat = acc[:, :, :].rearrange("p b c -> p (b c)")
                        at = []

                        def tile(i, s):
                            if s % 2 == 0:
                                e.load(regs, btab[0:1, bass.ds((RS * i + s) * (RG // U), 2 * RG // U)])
                                at[:] = [e.snap(r, min_val=0, max_val=(NB - 1) * AW) for r in regs]
                            e.wait_ge(oh_ready, RS * i + s + 1)
                            e.wait_ge(lowp, RS * i + s + 1)
                            for g in range(RG):
                                for k in range(3):
                                    mm = e.matmul(flat[:, bass.ds(at[(s % 2 * RG + g) // U], RW)],
                                                  onehot[:, s % ROH, :, g],
                                                  part[:, s, k, g, :], start=False, stop=False,
                                                  skip_group_check=True)
                            mm.then_inc(used, 1)
                        with only(e, general):
                            for b in range(7):
                                e.matmul(acc[:, b, :], zero16[:, 0:P], zero16[:, :], start=True, stop=False,
                                         skip_group_check=True)
                            e.wait_ge(bt_in, 16)
                            over_tiles(e, RT, RS, (tile, 0))
                            for b in range(7):
                                mm = e.matmul(acc[:, b, :], zero16[:, 0:P], zero16[:, :], start=False,
                                              stop=True, skip_group_check=True)
                            mm.then_inc(summed, 1)

        def center(e, done, val, mean, centred):
            done(e.tensor_reduce(mean, val, AX.X, ALU.add))
            done(e.tensor_scalar(mean, mean, 1.0 / C, None, ALU.mult))
            e.tensor_tensor(val, val, bc_last(mean, C), ALU.subtract).then_inc(centred, 1)

        def variance(e, done, squares, var, ask):
            done(e.tensor_reduce(var, squares, AX.X, ALU.add))
            e.tensor_scalar(var, var, 1.0 / C, EPS, ALU.mult, ALU.add).then_inc(ask, 1)

        agg_ctx = ExitStack()
        accT = sb("accT", [C, NN + P], F32, agg_ctx)
        far_places(0, dst_i, perm0, "a")
        with ExitStack() as ph:
            slot = sb("slot0", [P, SLOTS, G, EM + RW], F32, ph)
            gidx = sb("gidx0", [P, SLOTS, G], I32, ph)
            sidx = sb("sidx0", [P, SLOTS, G], I32, ph)
            ecomp = sb("ecomp0", [P, SLOTS, G * EM], F32, ph)
            onehot = sb("onehot0", [P, SLOTS, G, P], F32, ph)
            key = sb("key_s", [P, K], F32, ph)
            key_i = sb("key_is", [P, K], I32, ph)
            mask = sb("mask_s", [P, K], U16, ph)
            run = sb("run_s", [P, K], F32, ph)
            pos = sb("pos_s", [P, K], F32, ph)
            sums = ps("sums0", [P, SLOTS, 512], F32, ph)
            gathered = [sem(f"gathered{s}a", ph) for s in range(SLOTS)]
            scattered = [sem(f"scattered{s}a", ph) for s in range(SLOTS)]
            estored = [sem(f"estored{s}a", ph) for s in range(SLOTS)]
            idx_ready, lo_ready, compact, oh_ready, summed, added, v, turn_done, conv, sq = (
                sem(n + "a", ph) for n in ("idx_ready", "lo_ready", "compact", "oh_ready_n", "summed_n",
                                           "added", "vp", "turn_p", "conv", "sq"))
            starts = Starts(1, src_cnt, perm1, "s", ph)
            with nc.Block() as block:
                @block.vector
                def _(e):
                    steps = [0]

                    def done(ins):
                        ins.then_inc(v, 1)
                        steps[0] += 1
                        e.wait_ge(v, steps[0])

                    def indices(i, s, far):
                        cols = bass.ds((SLOTS * i + s) * G, G)
                        if not first_turn(i):
                            e.wait_ge((scattered if far else gathered)[s], 16 * G * i)
                        e.tensor_copy(gidx[:, s, :], src_i[:, cols]).then_inc(idx_ready, 1)
                        if far:
                            e.tensor_copy(sidx[:, s, :], pos_i[:, cols]).then_inc(idx_ready, 1)
                            e.tensor_copy(slot[:, s, :, EM + C], key[:, cols]).then_inc(idx_ready, 1)

                    def near_onehot(i, s):
                        if not first_turn(i):
                            e.wait_ge(summed, SLOTS * (i - 1) + s + 1)
                        e.tensor_tensor(onehot[:, s], bc_mid(iota_f[:, :], G),
                                        bc_last(d_off[:, bass.ds((SLOTS * i + s) * G, G)], P),
                                        ALU.is_equal).then_inc(oh_ready, 1)

                    def add_window(i, s):
                        t = SLOTS * i + s
                        first = e.value_load(win_i[0:1, bass.ds(t, 1)], min_val=0, max_val=NN - 1)
                        e.wait_ge(summed, t + 1)
                        if not first_turn(i) or t > 0:
                            e.wait_ge(added, t)
                        at = accT[:, bass.ds(first, P)]
                        e.tensor_tensor(at, at, sums[0:C, s, 0:P], ALU.add).then_inc(added, 1)

                    def cutoff():
                        rounded, turns, whole = pos, run, key_i
                        e.tensor_scalar(turns[:, :], weight[:, :], 1.0 / (2 * CUTOFF), None,
                                        ALU.mult).then_inc(conv, 1)
                        e.wait_ge(conv, 1)
                        e.tensor_copy(whole[:, :], turns[:, :]).then_inc(conv, 1)
                        e.wait_ge(conv, 2)
                        e.tensor_copy(rounded[:, :], whole[:, :]).then_inc(conv, 1)
                        e.wait_ge(conv, 3)
                        e.tensor_tensor(turns[:, :], turns[:, :], rounded[:, :], ALU.subtract).then_inc(conv, 1)
                        e.wait_ge(sq, 1)
                        e.tensor_tensor(turns[:, :], turns[:, :], turns[:, :], ALU.mult).then_inc(sq, 1)
                        e.wait_ge(sq, 2)
                        e.tensor_scalar(turns[:, :], turns[:, :], -1.0, 1.0, ALU.mult, ALU.add).then_inc(sq, 1)
                        e.wait_ge(sq, 3)
                        e.scalar_tensor_tensor(weight[:, :], weight[:, :], CUTOFF, turns[:, :], ALU.is_lt,
                                               ALU.mult).then_inc(sq, 1)
                        e.wait_ge(sq, 4)

                    e.memset(slot[:, :, :, EM + C:EM + RW], 0.0).then_inc(lo_ready, 1)
                    e.wait_ge(lo_ready, 1)
                    is_near = e.value_load(near[0:1, 0:1], min_val=0, max_val=1)
                    with e.If(is_near == 0):
                        cutoff()
                        done(e.tensor_scalar(key_i[:, :], dst_i[:, :], P - 1, None, ALU.bitwise_and))
                        done(e.tensor_copy(key[:, :], key_i[:, :]))
                        over_tiles(e, NT, SLOTS, (lambda i, s: indices(i, s, True), 0))
                        steps[0] = 0
                    with e.If(is_near == 1):
                        def clear_sums_and_weigh():
                            done(e.memset(accT[:, :], 0.0))
                            cutoff()

                        def prepare_places():
                            starts.vector(e)
                            done(e.tensor_scalar(key_i[:, :], src_i[:, :], 7, None, ALU.logical_shift_right))
                            done(e.tensor_copy(key[:, :], key_i[:, :]))
                            done(e.memset(pos[:, :], 0.0))

                        def place(turn):
                            own = [0]

                            def in_turn(ins):
                                ins.then_inc(turn_done, 1)
                                own[0] += 1
                                e.wait_ge(turn_done, 3 * PB * (turn - 1) + own[0])
                                e.sem_inc(passed, 1)
                            for b in range(PB):
                                place_bucket(e, PB * (turn - 1) + b, (key, mask, run, pos), in_turn)
                        over_tiles(e, NT, SLOTS, (lambda i, s: indices(i, s, False), 0), (near_onehot, 0),
                                   (add_window, 2), beside=place,
                                   after={1: clear_sums_and_weigh, 3: prepare_places, NT - 1: lambda:
                                          rows_of_places(e, pos, key_i, run[:, :].bitcast(I32), done)})

                @block.tensor
                def _(e):
                    def tile(i, s):
                        t = SLOTS * i + s
                        e.wait_ge(gathered[s], 16 * G * (i + 1))
                        e.wait_ge(oh_ready, t + 1)
                        if not first_turn(i):
                            e.wait_ge(added, SLOTS * (i - 1) + s + 1)
                        for g in range(G):
                            mm = e.matmul(sums[0:C, s, 0:P], slot[:, s, g, EM:EM + C], onehot[:, s, g, :],
                                          start=(g == 0), stop=(g == G - 1))
                        mm.then_inc(summed, 1)
                    is_near = e.value_load(near[0:1, 0:1], min_val=0, max_val=1)
                    with e.If(is_near == 1):
                        starts.tensor(e)
                        over_tiles(e, NT, SLOTS, (tile, 0))

                @block.scalar
                def _(e):
                    e.wait_ge(conv, 4)
                    e.activation(run[:, :], run[:, :], ACT.Sin, scale=3.1415925).then_inc(sq, 1)

                    def compact_rows(i, s):
                        e.wait_ge(gathered[s], 16 * G * (i + 1))
                        if not first_turn(i):
                            e.wait_ge(estored[s], 16 * i)
                        e.activation(ecomp[:, s, :].rearrange("p (g c) -> p g c", c=EM),
                                     slot[:, s, :, 0:EM], ACT.Copy).then_inc(compact, 1)
                    over_tiles(e, NT, SLOTS, (compact_rows, 0))

                @block.sync
                def _(e):
                    def store(i, s):
                        t = SLOTS * i + s
                        e.wait_ge(compact, t + 1)
                        e.dma_start(src_emb[:, bass.ds(t * (G * EM), G * EM)], ecomp[:, s, :]
                                    ).then_inc(estored[s], 16)
                    def clear_some(turn):
                        for b in range(PB):
                            starts.clear_last(e, PB * (turn - 1) + b)

                    is_near = e.value_load(near[0:1, 0:1], min_val=0, max_val=1)
                    with e.If(is_near == 1):
                        starts.clear_tail(e)
                        over_tiles(e, NT, SLOTS, (store, 0), beside=clear_some)
                        starts.store(e, SW)
                    with e.If(is_near == 0):
                        over_tiles(e, NT, SLOTS, (store, 0))
                    for s in range(SLOTS):
                        e.wait_ge(estored[s], 16 * tiles_of(s, NT, SLOTS))

                @block.gpsimd
                def _(e):
                    def gather(i, s, far):
                        t = SLOTS * i + s
                        if not first_turn(i):
                            e.wait_ge(compact, t - SLOTS + 1)
                            if not far:
                                e.wait_ge(summed, t - SLOTS + 1)
                        wait_apart(e, idx_ready, (3 if far else 1) * (t + 1), passed)
                        for g in range(G):
                            e.indirect_dma_start(out=slot[:, s, g, 0:EM + C], out_offset=None, in_=table0,
                                                 in_offset=bass.IndirectOffsetOnAxis(ap=gidx[:, s, g:g + 1],
                                                                                     axis=0)
                                                 ).then_inc(gathered[s], 16)

                    def scatter(i, s):
                        wait_apart(e, gathered[s], 16 * G * (i + 1), passed)
                        for g in range(G):
                            e.indirect_dma_start(out=perm0,
                                                 out_offset=bass.IndirectOffsetOnAxis(ap=sidx[:, s, g:g + 1],
                                                                                      axis=0),
                                                 in_=slot[:, s, g, EM:EM + RW], in_offset=None
                                                 ).then_inc(scattered[s], 16)

                    starts.pool(e)
                    e.wait_ge(lo_ready, 1)
                    is_near = e.value_load(near[0:1, 0:1], min_val=0, max_val=1)
                    with e.If(is_near == 1):
                        over_tiles(e, NT, SLOTS, (lambda i, s: gather(i, s, False), 0))
                        for s in range(SLOTS):
                            e.wait_ge(gathered[s], 16 * G * tiles_of(s, NT, SLOTS))
                    with e.If(is_near == 0):
                        over_tiles(e, NT, SLOTS, (lambda i, s: gather(i, s, True), 0), (scatter, 1))
                        for s in range(SLOTS):
                            e.wait_ge(scattered[s], 16 * G * tiles_of(s, NT, SLOTS))

        agg = sb("agg0", [P, NB, RW], F32, agg_ctx)
        reduce_rows(0, perm0, agg, "a", True)
        with ExitStack() as ph:
            tmp = sb("tmp0", [P, NB, C], F32, ph)
            tab = sb("tab1", [P, NB, TW], F32, ph)
            rest = sb("rest1", [P, NB, TW], F32, ph)
            prt = sb("prt1", [P, NB, PW], BF16, ph)
            mean, var = sb("mean0", [P, NB], F32, ph), sb("var0", [P, NB], F32, ph)
            expo = sb("expo0", [P, NB], F32, ph)
            back = ps("back", [P, 2, 512], F32, ph)
            (turned, taken, v, centred, squared, ask, answer, typed, tabbed, highs, rested, mids, lows, padded,
             stored) = (
                sem(n, ph) for n in ("turned_t", "taken_t", "v0", "centred0", "squared0", "ask0", "answer0",
                                     "typed0", "tabbed0", "highs0", "rested0", "mids0", "lows0", "padded0",
                                     "stored0"))
            with nc.Block() as block:
                @block.tensor
                def _(e):
                    is_near = e.value_load(near[0:1, 0:1], min_val=0, max_val=1)
                    with e.If(is_near == 1):
                        for b in range(7):
                            if b >= 2:
                                e.wait_ge(taken, b - 1)
                            for k in range(min(8, NB - 8 * b)):
                                h = 8 * b + k
                                mm = e.transpose(back[:, b % 2, C * k:C * (k + 1)], accT[:, P * h:P * (h + 1)],
                                                 ident[0:C, 0:C])
                            mm.then_inc(turned, 1)

                @block.vector
                def _(e):
                    steps = [0]

                    def done(ins):
                        ins.then_inc(v, 1)
                        steps[0] += 1
                        e.wait_ge(v, steps[0])
                    is_near = e.value_load(near[0:1, 0:1], min_val=0, max_val=1)
                    done(e.memset(expo[:, :], -0.5))
                    done(e.tensor_tensor(tmp[:, :, :], x1[:, :, :], bc_last(dinv[:, :], C), ALU.mult))
                    with e.If(is_near == 1):
                        for b in range(7):
                            at = tmp[:, 8 * b:min(8 * b + 8, NB), :]
                            e.wait_ge(turned, b + 1)
                            e.tensor_tensor(at, at, back[:, b % 2, 0:C * at.shape[1]].rearrange(
                                "p (k c) -> p k c", c=C), ALU.add).then_inc(taken, 1)
                        e.wait_ge(taken, 7)
                    with e.If(is_near == 0):
                        e.tensor_tensor(tmp[:, :, :], tmp[:, :, :], agg[:, :, 0:C], ALU.add).then_inc(taken, 7)
                        e.wait_ge(taken, 7)

                    def update(k, a, b):
                        t, xs = tmp[:, a:b, :], x1[:, a:b, :]
                        done(e.tensor_tensor(t, t, bc_last(dinv[:, a:b], C), ALU.mult))
                        done(e.tensor_tensor(xs, xs, t, ALU.add))
                        center(e, done, xs, mean[:, a:b], centred)

                    def spread(k, a, b):
                        e.wait_ge(squared, k + 1)
                        variance(e, done, tmp[:, a:b, :], var[:, a:b], ask)

                    def second_table(k, a, b):
                        xs = x1[:, a:b, :]
                        e.wait_ge(answer, k + 1)
                        done(e.tensor_tensor(xs, xs, bc_last(mean[:, a:b], C), ALU.mult))
                        e.tensor_tensor(tab[:, a:b, EM:EM + C], xs, bc_last(nv[:, a:b], C),
                                        ALU.mult).then_inc(tabbed, 1)

                    def less_high(k, a, b):
                        e.wait_ge(highs, k + 1)
                        e.tensor_tensor(rest[:, a:b, :], tab[:, a:b, :], prt[:, a:b, 0:TW],
                                        ALU.subtract).then_inc(rested, 1)

                    def less_middle(k, a, b):
                        e.wait_ge(mids, k + 1)
                        e.tensor_tensor(prt[:, a:b, 2 * TW:3 * TW], rest[:, a:b, :], prt[:, a:b, TW:2 * TW],
                                        ALU.subtract).then_inc(lows, 1)
                    in_waves(update, spread, second_table, less_high, less_middle)

                @block.scalar
                def _(e):
                    e.activation(tab[:, :, 0:EM], type_e[:, :, EM:2 * EM], ACT.Copy).then_inc(typed, 1)
                    e.activation(tab[:, :, EM + C], nv[:, :], ACT.Copy).then_inc(typed, 1)
                    e.wait_ge(typed, 2)

                    def square(k, a, b):
                        e.wait_ge(centred, k + 1)
                        e.activation(tmp[:, a:b, :], x1[:, a:b, :], ACT.Square).then_inc(squared, 1)

                    def high_part(k, a, b):
                        e.wait_ge(tabbed, k + 1)
                        e.activation(prt[:, a:b, 0:TW], tab[:, a:b, :], ACT.Copy).then_inc(highs, 1)

                    def middle_part(k, a, b):
                        e.wait_ge(rested, k + 1)
                        e.activation(prt[:, a:b, TW:2 * TW], rest[:, a:b, :], ACT.Copy).then_inc(mids, 1)
                    in_waves(square, None, high_part, middle_part)

                @block.gpsimd
                def _(e):
                    e.memset(prt[:, :, 3 * TW:PW], 0.0).then_inc(padded, 1)
                    for k, (a, b) in enumerate(PARTS):
                        e.wait_ge(ask, k + 1)
                        e.tensor_tensor(mean[:, a:b], var[:, a:b], expo[:, a:b], ALU.pow).then_inc(answer, 1)

                @block.sync
                def _(e):
                    e.wait_ge(padded, 1)
                    for k, (a, b) in enumerate(PARTS):
                        e.wait_ge(lows, k + 1)
                        e.dma_start(parts1[P * a:P * b, :].rearrange("(h l) c -> l h c", l=P),
                                    prt[:, a:b, :]).then_inc(stored, 16)
                    with only(e, True):
                        e.dma_start(table1.rearrange("(h l) c -> l h c", l=P), tab[:, :, :]
                                    ).then_inc(stored, 16)
                        e.wait_ge(stored, 16 * len(PARTS) + 16)
                    e.wait_ge(stored, 16 * len(PARTS))
        agg_ctx.close()

        far_places(1, src_i, perm1, "b")
        with ExitStack() as ph:
            ea = sb("ea", [P, SLOTS, G * RA], F32, ph)
            es = sb("es", [P, SLOTS, G * EM], F32, ph)
            win = sb("win", [P, SLOTS, PW], BF16, ph)
            got = sb("got", [P, SLOTS, G, TW], F32, ph)
            msg = sb("msg", [P, SLOTS, G, RW], F32, ph)
            gidx = sb("gidx1", [P, SLOTS, G], I32, ph)
            sidx = sb("sidx1", [P, SLOTS, G], I32, ph)
            onehot = sb("onehot1", [P, SLOTS, P, G], BF16, ph)
            turned_oh = sb("turned_oh", [P, 2, HG, P], BF16, ph)
            ea_t = sb("ea_t", [2 * RA, 2, 512], F32, ph)
            hid = sb("hid", [2 * C + 1, 2, 512], F32, ph)
            prod = sb("prod", [P, G, EM], F32, ph)
            logit = sb("logit", [P, G], F32, ph)
            val = sb("val", [P, 2, HG, C], F32, ph)
            poh = ps("poh", [P, 2, HG, P], BF16, ph)
            pt = ps("pt", [2 * RA, 512], F32, ph)
            phid = ps("phid", [2 * C, 512], F32, ph)
            gate = ps("gate", [P, 2, 512], F32, ph)
            pwin = ps("pwin", [P, 2, 512], F32, ph)
            gathered = [sem(f"gathered{s}b", ph) for s in range(SLOTS)]
            scattered = [sem(f"scattered{s}b", ph) for s in range(SLOTS)]
            ea_in = [sem(f"ea_in{s}", ph) for s in range(SLOTS)]
            (idx_ready, ones_ready, turned, turned_sb, hidden, hidden_sb, gated, gate_used, msg_ready, own,
             oh_ready, oh_turned, oh_sb, picked, picked_sb) = (
                sem(n + "b", ph) for n in ("idx_ready", "ones_ready", "turned", "turned_sb", "hidden",
                                           "hidden_sb", "gated", "gate_used", "msg_ready", "own", "oh_ready",
                                           "oh_turned", "oh_sb", "picked", "picked_sb"))

            def both_ways(e, program):
                flag = e.value_load(near[0:1, 0:1], min_val=0, max_val=1)
                with e.If(flag == 1):
                    program(True)
                with e.If(flag == 0):
                    program(False)

            def halves(i, s, hf):
                return 2 * (SLOTS * i + s) + hf

            def later(i, n, least):
                return not first_turn(i) or n >= least

            with nc.Block() as block:
                @block.sync
                def _(e):
                    def program(is_near):
                        def load(i, s):
                            t = SLOTS * i + s
                            if is_near:
                                first = e.value_load(win_i[0:1, bass.ds(t, 1)], min_val=0, max_val=NN - 1)
                            if not first_turn(i):
                                e.wait_ge(msg_ready, 4 * (t - SLOTS + 1))
                            e.dma_start(ea[:, s, :], edge_attr[bass.ds(t, 1)].rearrange("o p c -> (o p) c")
                                        ).then_inc(ea_in[s], 16)
                            e.dma_start(es[:, s, :], src_emb[:, bass.ds(t * (G * EM), G * EM)]
                                        ).then_inc(ea_in[s], 16)
                            if is_near:
                                e.dma_start(win[:, s, :], parts1[bass.ds(first, P), :]).then_inc(ea_in[s], 16)
                        over_tiles(e, NT, SLOTS, (load, 0))
                    both_ways(e, program)

                @block.tensor
                def _(e):
                    e.wait_ge(ones_ready, 1)

                    def program(is_near):
                        def turn_onehots(i, s, hf):
                            n = halves(i, s, hf)
                            if later(i, n, 2):
                                e.wait_ge(oh_sb, n - 1)
                            for g in range(HG):
                                mm = e.transpose(poh[:, hf, g, :], onehot[:, s, :, hf * HG + g], ident16[:, :])
                            mm.then_inc(oh_turned, 1)

                        def turn_attributes(i, s, hf):
                            n = halves(i, s, hf)
                            if later(i, n, 1):
                                e.wait_ge(turned_sb, n)
                            for k in range(4):
                                g = hf * HG + 2 * k
                                mm = e.transpose(pt[:, P * k:P * (k + 1)], ea[:, s, g * RA:(g + 2) * RA],
                                                 ident[:, :])
                            mm.then_inc(turned, 1)

                        def hidden_layer(i, s, hf):
                            n = halves(i, s, hf)
                            e.wait_ge(turned_sb, n + 1)
                            if later(i, n, 1):
                                e.wait_ge(hidden_sb, n)
                            e.matmul(phid[:, :], w1[:, :], ea_t[:, hf, :], start=True,
                                     stop=True).then_inc(hidden, 1)

                        def pick_rows(i, s, hf):
                            n = halves(i, s, hf)
                            e.wait_ge(oh_sb, n + 1)
                            if later(i, n, 1):
                                e.wait_ge(picked_sb, n)
                            for g in range(HG):
                                at = pwin[:, g // 4, TW * (g % 4):TW * (g % 4 + 1)]
                                for k in range(3):
                                    mm = e.matmul(at, turned_oh[:, hf, g, :], win[:, s, TW * k:TW * (k + 1)],
                                                  start=(k == 0), stop=(k == 2))
                            mm.then_inc(picked, 1)

                        def gates(i, s, hf):
                            n = halves(i, s, hf)
                            e.wait_ge(hidden_sb, n + 1)
                            if later(i, n, 2):
                                e.wait_ge(gate_used, n - 1)
                            for k in range(4):
                                mm = e.matmul(gate[:, hf, 2 * C * k:2 * C * (k + 1)],
                                              hid[:, hf, P * k:P * (k + 1)], w2[:, :], start=True, stop=True)
                            mm.then_inc(gated, 1)

                        def tile(i, s):
                            e.wait_ge(ea_in[s], (48 if is_near else 32) * (i + 1))
                            if is_near:
                                e.wait_ge(oh_ready, SLOTS * i + s + 1)
                                turn_onehots(i, s, 0)
                                turn_onehots(i, s, 1)
                            turn_attributes(i, s, 0)
                            hidden_layer(i, s, 0)
                            turn_attributes(i, s, 1)
                            if is_near:
                                pick_rows(i, s, 0)
                            hidden_layer(i, s, 1)
                            gates(i, s, 0)
                            if is_near:
                                pick_rows(i, s, 1)
                            gates(i, s, 1)
                        over_tiles(e, NT, SLOTS, (tile, 0))
                    both_ways(e, program)

                @block.scalar
                def _(e):
                    def program(is_near):
                        def copy_onehots(i, s, hf):
                            n = halves(i, s, hf)
                            e.wait_ge(oh_turned, n + 1)
                            if later(i, n, 2):
                                e.wait_ge(picked, n - 1)
                            e.activation(turned_oh[:, hf], poh[:, hf], ACT.Copy).then_inc(oh_sb, 1)

                        def copy_attributes(i, s, hf):
                            n = halves(i, s, hf)
                            e.wait_ge(turned, n + 1)
                            if later(i, n, 2):
                                e.wait_ge(hidden, n - 1)
                            e.activation(ea_t[:, hf, :], pt[:, :], ACT.Copy).then_inc(turned_sb, 1)

                        def silu(i, s, hf):
                            n = halves(i, s, hf)
                            e.wait_ge(hidden, n + 1)
                            if later(i, n, 2):
                                e.wait_ge(gated, n - 1)
                            e.activation(hid[0:2 * C, hf, :], phid[:, :], ACT.Silu,
                                         bias=b1c[:, 0:1]).then_inc(hidden_sb, 1)

                        def copy_rows(i, s, hf):
                            n = halves(i, s, hf)
                            e.wait_ge(picked, n + 1)
                            if not first_turn(i):
                                e.wait_ge(msg_ready, 4 * (SLOTS * (i - 1) + s + 1))
                            rows = pwin[:, :, 0:4 * TW].rearrange("p b (k c) -> p b k c", c=TW)
                            e.activation(got[:, s, hf * HG:(hf + 1) * HG, :].rearrange(
                                "p (b k) c -> p b k c", b=2), rows, ACT.Copy).then_inc(picked_sb, 1)

                        def tile(i, s):
                            if is_near:
                                copy_onehots(i, s, 0)
                            copy_attributes(i, s, 0)
                            if is_near:
                                copy_onehots(i, s, 1)
                            silu(i, s, 0)
                            copy_attributes(i, s, 1)
                            if is_near:
                                copy_rows(i, s, 0)
                            silu(i, s, 1)
                            if is_near:
                                copy_rows(i, s, 1)
                        over_tiles(e, NT, SLOTS, (tile, 0))
                    both_ways(e, program)

                @block.vector
                def _(e):
                    e.memset(hid[2 * C:2 * C + 1, :, :], 1.0).then_inc(ones_ready, 1)

                    def program(is_near):
                        def indices(i, s):
                            t = SLOTS * i + s
                            cols = bass.ds(t * G, G)
                            if not first_turn(i):
                                e.wait_ge(scattered[s], 16 * G * i)
                            e.tensor_copy(sidx[:, s, :], pos_i[:, cols]).then_inc(idx_ready, 1)
                            if not is_near:
                                e.tensor_copy(gidx[:, s, :], dst_i[:, cols]).then_inc(idx_ready, 1)

                        def onehots(i, s):
                            t = SLOTS * i + s
                            if not first_turn(i):
                                e.wait_ge(oh_turned, 2 * (t - SLOTS + 1))
                            e.tensor_tensor(onehot[:, s], number[:, :, :],
                                            bc_mid(d_off[:, bass.ds(t * G, G)], P),
                                            ALU.is_equal).then_inc(oh_ready, 1)

                        def messages(i, s):
                            t = SLOTS * i + s
                            cols = bass.ds(t * G, G)
                            e.wait_ge(ea_in[s], (48 if is_near else 32) * (i + 1))
                            if is_near:
                                e.wait_ge(picked_sb, 2 * (t + 1))
                            else:
                                e.wait_ge(gathered[s], 16 * G * (i + 1))
                            own0 = 4 * t
                            e.tensor_tensor(prod[:, :, :], es[:, s, :].rearrange("p (g c) -> p g c", c=EM),
                                            got[:, s, :, 0:EM], ALU.mult).then_inc(own, 1)
                            e.wait_ge(own, own0 + 1)
                            e.tensor_reduce(logit[:, :], prod[:, :, :], AX.X, ALU.add).then_inc(own, 1)
                            e.wait_ge(own, own0 + 2)
                            for hf in range(2):
                                gs = slice(hf * HG, (hf + 1) * HG)
                                e.wait_ge(gated, 2 * t + hf + 1)
                                e.tensor_tensor(val[:, hf], gate[:, hf, 0:HG * C].rearrange(
                                    "p (g c) -> p g c", c=C), bc_last(logit[:, gs], C),
                                    ALU.add).then_inc(gate_used, 1)
                            e.wait_ge(gate_used, 2 * t + 2)
                            for hf in range(2):
                                gs = slice(hf * HG, (hf + 1) * HG)
                                e.tensor_tensor(val[:, hf], val[:, hf], got[:, s, gs, EM:EM + C],
                                                ALU.mult).then_inc(own, 1)
                            e.wait_ge(own, own0 + 4)
                            if not first_turn(i):
                                e.wait_ge(scattered[s], 16 * G * i)
                            for hf in range(2):
                                gs = slice(hf * HG, (hf + 1) * HG)
                                e.tensor_tensor(msg[:, s, gs, 0:C], val[:, hf],
                                                bc_last(weight[:, bass.ds(t * G + hf * HG, HG)], C),
                                                ALU.mult).then_inc(msg_ready, 1)
                            e.tensor_copy(msg[:, s, :, C], src_lo[:, cols]).then_inc(msg_ready, 1)
                            e.tensor_copy(msg[:, s, :, C + 1], got[:, s, :, EM + C]).then_inc(msg_ready, 1)
                            e.wait_ge(msg_ready, 4 * t + 2)

                        if is_near:
                            over_tiles(e, NT, SLOTS, (onehots, 0), (indices, 1), (messages, 1))
                        else:
                            over_tiles(e, NT, SLOTS, (indices, 0), (messages, 1))
                    both_ways(e, program)

                @block.gpsimd
                def _(e):
                    def program(is_near):
                        def gather(i, s):
                            wait_apart(e, idx_ready, 2 * (SLOTS * i + s + 1), passed)
                            for g in range(G):
                                e.indirect_dma_start(out=got[:, s, g, :], out_offset=None, in_=table1,
                                                     in_offset=bass.IndirectOffsetOnAxis(
                                                         ap=gidx[:, s, g:g + 1], axis=0)
                                                     ).then_inc(gathered[s], 16)

                        def scatter(i, s):
                            t = SLOTS * i + s
                            e.wait_ge(idx_ready, (1 if is_near else 2) * (t + 1))
                            wait_apart(e, msg_ready, 4 * (t + 1), passed)
                            for g in range(G):
                                e.indirect_dma_start(out=perm1,
                                                     out_offset=bass.IndirectOffsetOnAxis(
                                                         ap=sidx[:, s, g:g + 1], axis=0),
                                                     in_=msg[:, s, g, :], in_offset=None
                                                     ).then_inc(scattered[s], 16)
                        if is_near:
                            over_tiles(e, NT, SLOTS, (scatter, 0))
                        else:
                            over_tiles(e, NT, SLOTS, (gather, 0), (scatter, 2))
                        for s in range(SLOTS):
                            e.wait_ge(scattered[s], 16 * G * tiles_of(s, NT, SLOTS))
                    both_ways(e, program)

        with ExitStack() as ph:
            agg = sb("agg1", [P, NB, RW], F32, ph)
            reduce_rows(1, perm1, agg, "b", False)
            tmp = sb("tmp1", [P, NB, C], F32, ph)
            y = sb("y1", [P, NB, C], F32, ph)
            x_bet = sb("x_bet", [P, NB, C], F32, ph)
            mean, var = sb("mean1", [P, NB], F32, ph), sb("var1", [P, NB], F32, ph)
            expo = sb("expo1", [P, NB], F32, ph)
            v, shifted, ready, stored = (sem(n, ph) for n in ("v1", "shifted1", "ready1", "stored1"))
            centred, squared, ask, answer = ([sem(n + k, ph) for k in ("x", "y")] for n in (
                "centred1", "squared1", "ask1", "answer1"))
            with nc.Block() as block:
                @block.vector
                def _(e):
                    steps = [0]

                    def done(ins):
                        ins.then_inc(v, 1)
                        steps[0] += 1
                        e.wait_ge(v, steps[0])
                    done(e.memset(expo[:, :], -0.5))
                    done(e.tensor_scalar(var[:, :], agg[:, :, C + 1], 1e-8, None, ALU.max))
                    done(e.reciprocal(mean[:, :], var[:, :]))

                    def average(k, a, b):
                        ys = y[:, a:b, :]
                        done(e.tensor_tensor(ys, agg[:, a:b, 0:C], bc_last(mean[:, a:b], C), ALU.mult))
                        done(e.tensor_tensor(ys, ys, x1[:, a:b, :], ALU.add))
                        center(e, done, ys, mean[:, a:b], centred[0])

                    def spread(norm):
                        def step(k, a, b):
                            e.wait_ge(squared[norm], k + 1)
                            variance(e, done, tmp[:, a:b, :], var[:, a:b], ask[norm])
                        return step

                    def residual(k, a, b):
                        ys = y[:, a:b, :]
                        e.wait_ge(answer[0], k + 1)
                        done(e.tensor_tensor(ys, ys, bc_last(mean[:, a:b], C), ALU.mult))
                        done(e.tensor_tensor(ys, ys, bc_mid(gam[:, :], b - a), ALU.mult))
                        e.wait_ge(shifted, 1)
                        done(e.tensor_tensor(ys, ys, x_bet[:, a:b, :], ALU.add))
                        center(e, done, ys, mean[:, a:b], centred[1])

                    def scale(k, a, b):
                        ys = y[:, a:b, :]
                        e.wait_ge(answer[1], k + 1)
                        e.tensor_tensor(ys, ys, bc_last(mean[:, a:b], C), ALU.mult).then_inc(ready, 1)
                    in_waves(average, spread(0), residual, spread(1), scale)

                @block.scalar
                def _(e):
                    def square(norm):
                        def step(k, a, b):
                            e.wait_ge(centred[norm], k + 1)
                            e.activation(tmp[:, a:b, :], y[:, a:b, :], ACT.Square).then_inc(squared[norm], 1)
                        return step
                    in_waves(square(0), None, square(1))

                @block.gpsimd
                def _(e):
                    e.tensor_tensor(x_bet[:, :, :], x1[:, :, :], bc_mid(bet[:, :], NB), ALU.add
                                    ).then_inc(shifted, 1)

                    def inverse_root(norm):
                        def step(k, a, b):
                            e.wait_ge(ask[norm], k + 1)
                            e.tensor_tensor(mean[:, a:b], var[:, a:b], expo[:, a:b],
                                            ALU.pow).then_inc(answer[norm], 1)
                        return step
                    in_waves(None, inverse_root(0), None, inverse_root(1))

                @block.sync
                def _(e):
                    full = NODES // P
                    for k, (a, b) in enumerate(PARTS):
                        e.wait_ge(ready, k + 1)
                        b = min(b, full)
                        e.dma_start(out[a * P:b * P, :].rearrange("(h l) c -> l h c", l=P),
                                    y[:, a:b, :]).then_inc(stored, 16)
                    e.dma_start(out[full * P:NODES, :], y[0:NODES - full * P, full, :]).then_inc(stored, 16)
                    e.wait_ge(stored, 16 * len(PARTS) + 16)


def kernel(**inputs):
    import numpy as np
    import concourse.bacc as bacc
    from concourse.bass_utils import run_bass_kernel_spmd

    a = {k: np.ascontiguousarray(v) for k, v in inputs.items()}

    def padded(v, n, fill=0):
        out = np.full((n,) + v.shape[1:], fill, v.dtype)
        out[:v.shape[0]] = v
        return out

    def by_tile(v, fill=0):
        return np.ascontiguousarray(padded(v, K * P, fill).reshape(NT, P, G).transpose(1, 0, 2).reshape(P, K))

    def by_node(v):
        return np.ascontiguousarray(padded(v, NN).reshape(NB, P).T)

    f = {
        "x": padded(a["x"], NN),
        "src": by_tile(a["src"], NN - 1),
        "dst": by_tile(a["dst"], NN - 1),
        "edge_attr": padded(a["edge_attr_40"], K * P).reshape(NT, P, G * RA),
        "edge_weight": by_tile(a["edge_weight"]),
        "node_type": by_node(a["node_type_119"]),
        "node_vec": by_node(a["node_vec"]),
        "W1T": np.ascontiguousarray(a["L1_gnn_W1"].T),
        "b1": a["L1_gnn_b1"].reshape(C, 1),
        "W2T": np.ascontiguousarray(a["L1_gnn_W2"].T),
        "b2": a["L1_gnn_b2"].reshape(1, C),
        "emb": a["L1_gnn_emb"],
        "embT": np.ascontiguousarray(a["L1_gnn_emb"].T),
        "adaptWT": np.ascontiguousarray(a["L1_gnn_adaptW"].T),
        "gamma": a["L1_gnn_gamma"].reshape(1, C),
        "beta": a["L1_gnn_beta"].reshape(1, C),
    }
    nc = bacc.Bacc("TRN2", target_bir_lowering=False, num_devices=1)
    args = {k: nc.dram_tensor("in_" + k, v.shape, mybir.dt.from_np(v.dtype), kind="ExternalInput").ap()
            for k, v in f.items()}
    out = nc.dram_tensor("out_nodes", (NODES, C), F32, kind="ExternalOutput").ap()
    build(nc, out=out, **args)
    r = run_bass_kernel_spmd(nc, [{"in_" + k: v for k, v in f.items()}], core_ids=[0])
    return r.results[0]["out_nodes"]
```
